# Optimizing a Trainium2 kernel written in Bass

```python
import numpy as np
import jax
import jax.numpy as jnp

def _softmax(x, axis=-1):
    return jax.nn.softmax(x, axis=axis)

def _gelu(x):
    return jax.nn.gelu(x, approximate=True)

def _silu(x):
    return jax.nn.silu(x)

def _sigmoid(x):
    return jax.nn.sigmoid(x)

def _layernorm(x, axis=-1, eps=1e-05):
    m = jnp.mean(x, axis=axis, keepdims=True)
    v = jnp.var(x, axis=axis, keepdims=True)
    return (x - m) / jnp.sqrt(v + eps)

def _scatter_add(tgt, idx, src, axis=0):
    return tgt.at[idx].add(src)

def _segment_sum(src, seg, n):
    return jax.ops.segment_sum(src, seg, n)
kernel_name = 'mk_decoder_preln_d1_seqx_r8_dcedff'

def setup_inputs(seed: int=0):
    np.random.seed(seed)
    _w = jnp.asarray

    def _rec_inputs():
        import jax
        import jax.numpy as jnp
        _rk = jax.random.key(seed)
        x = 0.0001212 + 1 * jax.random.normal(jax.random.fold_in(_rk, 1), (16, 128, 256), jnp.float32)
        _lenS = 128 - jax.random.randint(jax.random.fold_in(_rk, 7), (16,), 0, max(1, 128 // 4) + 1, jnp.int32)
        _lenS2 = 128 - jax.random.randint(jax.random.fold_in(_rk, 8), (16,), 0, max(1, 128 // 4) + 1, jnp.int32)
        _ctx_2048P = jax.random.normal(jax.random.fold_in(_rk, 11), (16, 16, 256), jnp.float32)
        _ctx_2048c = jax.random.dirichlet(jax.random.fold_in(_rk, 511), 0.3 * jnp.ones((16,), jnp.float32), (16, 128))
        _ctx_2048t = jnp.einsum('bsk,bkd->bsd', _ctx_2048c, _ctx_2048P)
        _ctx_2048t = _ctx_2048t * jax.lax.rsqrt(jnp.mean(jnp.square(_ctx_2048t)) + 1e-12) * 0.953939
        ctx_2048 = 0.000173663 + 1.0001 * (_ctx_2048t + 0.3 * jax.random.normal(jax.random.fold_in(_rk, 611), (16, 128, 256), jnp.float32))
        return (x, ctx_2048)
    x, ctx_2048 = _rec_inputs()

    def _L0_attn_setup():
        import jax, jax.numpy as jnp
        import numpy as np
        BATCH, SEQ, HID = (1, 256, 256)
        INTER, STATE, DT_RANK, KCONV = (512, 16, 128, 4)

        def _mamba_forward(input_states, in_proj_w, conv_w, conv_b, x_proj_w, dt_proj_w, dt_proj_b, A_log, D, out_proj_w):
            Bsz, L, _ = input_states.shape
            Idim, _, K = conv_w.shape
            N = A_log.shape[1]
            R = dt_proj_w.shape[0]
            proj = input_states @ in_proj_w
            hidden, gate = jnp.split(proj, 2, axis=-1)
            xc = jnp.swapaxes(hidden, 1, 2)
            xc = jax.lax.conv_general_dilated(xc, conv_w, window_strides=(1,), padding=((K - 1, K - 1),), feature_group_count=Idim)
            xc = xc[:, :, :L] + conv_b[None, :, None]
            u = jax.nn.silu(jnp.swapaxes(xc, 1, 2))
            ssm_in = u @ x_proj_w
            dt_in, Bc, Cc = jnp.split(ssm_in, [R, R + N], axis=-1)
            dt = jax.nn.softplus(dt_in @ dt_proj_w + dt_proj_b)
            A = -jnp.exp(A_log)

            def step(state, xs):
                dt_t, B_t, C_t, u_t = xs
                dA = jnp.exp(dt_t[:, :, None] * A[None])
                state = state * dA + (dt_t * u_t)[:, :, None] * B_t[:, None, :]
                y_t = jnp.einsum('bin,bn->bi', state, C_t)
                return (state, y_t)
            xs = (jnp.swapaxes(dt, 0, 1), jnp.swapaxes(Bc, 0, 1), jnp.swapaxes(Cc, 0, 1), jnp.swapaxes(u, 0, 1))
            state0 = jnp.zeros((Bsz, Idim, N), dt.dtype)
            _, ys = jax.lax.scan(step, state0, xs)
            y = jnp.swapaxes(ys, 0, 1)
            y = (y + u * D) * jax.nn.silu(gate)
            return y @ out_proj_w
        key = jax.random.key(seed)
        ks = jax.random.split(key, 8)
        f = jnp.float32
        return {'input_states': jax.random.normal(ks[0], (BATCH, SEQ, HID), f), 'in_proj_w': jax.random.normal(ks[1], (HID, 2 * INTER), f) * HID ** (-0.5), 'conv_w': jax.random.normal(ks[2], (INTER, 1, KCONV), f) * KCONV ** (-0.5), 'conv_b': jnp.zeros((INTER,), f), 'x_proj_w': jax.random.normal(ks[3], (INTER, DT_RANK + 2 * STATE), f) * INTER ** (-0.5), 'dt_proj_w': jax.random.normal(ks[4], (DT_RANK, INTER), f) * DT_RANK ** (-0.5), 'dt_proj_b': jax.random.normal(ks[5], (INTER,), f) * 0.1, 'A_log': jnp.log(jnp.broadcast_to(jnp.arange(1, STATE + 1, dtype=f), (INTER, STATE))), 'D': jnp.ones((INTER,), f), 'out_proj_w': jax.random.normal(ks[6], (INTER, HID), f) * INTER ** (-0.5)}
    _L0_attn_all = _L0_attn_setup()
    _L0_attn_in = {k: v for k, v in _L0_attn_all.items() if k in ('in_proj_w', 'conv_w', 'conv_b', 'x_proj_w', 'dt_proj_w', 'dt_proj_b', 'A_log', 'D', 'out_proj_w')}
    del _L0_attn_all

    def _L0_xattn_setup():
        import jax, jax.numpy as jnp
        import numpy as np
        B_DIM, T_DIM, C_DIM = (16, 128, 256)

        def _wkv(w, u, k, v):
            Bn, Tn, Cn = k.shape
            NEG_INF = jnp.float32(-1e+38)

            def step(carry, kv_t):
                p, q, o = carry
                kt, vt = kv_t
                no = jnp.maximum(o, u + kt)
                A = jnp.exp(o - no)
                E = jnp.exp(u + kt - no)
                y = (A * p + E * vt) / (A * q + E)
                no2 = jnp.maximum(w + o, kt)
                A2 = jnp.exp(w + o - no2)
                E2 = jnp.exp(kt - no2)
                return ((A2 * p + E2 * vt, A2 * q + E2, no2), y)
            init = (jnp.zeros((Bn, Cn), k.dtype), jnp.zeros((Bn, Cn), k.dtype), jnp.full((Bn, Cn), NEG_INF, k.dtype))
            kT = jnp.moveaxis(k, 1, 0)
            vT = jnp.moveaxis(v, 1, 0)
            _, yT = jax.lax.scan(step, init, (kT, vT))
            return jnp.moveaxis(yT, 0, 1)
        key = jax.random.key(seed)
        k1, k2, k3, k4 = jax.random.split(key, 4)
        w = -jnp.exp(jax.random.normal(k1, (C_DIM,), jnp.float32))
        u = jax.random.normal(k2, (C_DIM,), jnp.float32)
        k = jax.random.normal(k3, (B_DIM, T_DIM, C_DIM), jnp.float32)
        v = jax.random.normal(k4, (B_DIM, T_DIM, C_DIM), jnp.float32)
        return {'B': B_DIM, 'T': T_DIM, 'C': C_DIM, 'w': w, 'u': u, 'k': k, 'v': v}
    _L0_xattn_all = _L0_xattn_setup()
    _L0_xattn_in = {k: v for k, v in _L0_xattn_all.items() if k in ('w', 'u')}
    del _L0_xattn_all

    def _L0_ffn_setup():
        import jax, jax.numpy as jnp
        import numpy as np
        B, S, D_IN, D_OUT = (4, 256, 256, 256)
        EPS = 1e-10
        key = jax.random.key(seed)
        kx, kw, kb = jax.random.split(key, 3)
        x = jax.random.normal(kx, (B, S, D_IN), dtype=jnp.float32)
        weight = jax.random.normal(kw, (D_OUT, D_IN), dtype=jnp.float32) * 0.02
        bias = jax.random.normal(kb, (D_OUT,), dtype=jnp.float32) * 0.02
        return {'x': x, 'weight': weight, 'bias': bias}
    _L0_ffn_all = _L0_ffn_setup()
    _L0_ffn_in = {k: v for k, v in _L0_ffn_all.items() if k in ('weight', 'bias')}
    del _L0_ffn_all
    return {'x': x, 'ctx_2048': ctx_2048, 'L0_attn_in_proj_w': _L0_attn_in['in_proj_w'], 'L0_attn_conv_w': _L0_attn_in['conv_w'], 'L0_attn_conv_b': _L0_attn_in['conv_b'], 'L0_attn_x_proj_w': _L0_attn_in['x_proj_w'], 'L0_attn_dt_proj_w': _L0_attn_in['dt_proj_w'], 'L0_attn_dt_proj_b': _L0_attn_in['dt_proj_b'], 'L0_attn_A_log': _L0_attn_in['A_log'], 'L0_attn_D': _L0_attn_in['D'], 'L0_attn_out_proj_w': _L0_attn_in['out_proj_w'], 'L0_xattn_w': _L0_xattn_in['w'], 'L0_xattn_u': _L0_xattn_in['u'], 'L0_ffn_weight': _L0_ffn_in['weight'], 'L0_ffn_bias': _L0_ffn_in['bias']}

def reference(x, ctx_2048, L0_attn_in_proj_w, L0_attn_conv_w, L0_attn_conv_b, L0_attn_x_proj_w, L0_attn_dt_proj_w, L0_attn_dt_proj_b, L0_attn_A_log, L0_attn_D, L0_attn_out_proj_w, L0_xattn_w, L0_xattn_u, L0_ffn_weight, L0_ffn_bias):
    import jax
    import jax.numpy as jnp

    def _L0_attn_ref(input_states, in_proj_w, conv_w, conv_b, x_proj_w, dt_proj_w, dt_proj_b, A_log, D, out_proj_w):
        import jax, jax.numpy as jnp
        import numpy as np
        BATCH, SEQ, HID = (1, 256, 256)
        INTER, STATE, DT_RANK, KCONV = (512, 16, 128, 4)

        def _mamba_forward(input_states, in_proj_w, conv_w, conv_b, x_proj_w, dt_proj_w, dt_proj_b, A_log, D, out_proj_w):
            Bsz, L, _ = input_states.shape
            Idim, _, K = conv_w.shape
            N = A_log.shape[1]
            R = dt_proj_w.shape[0]
            proj = input_states @ in_proj_w
            hidden, gate = jnp.split(proj, 2, axis=-1)
            xc = jnp.swapaxes(hidden, 1, 2)
            xc = jax.lax.conv_general_dilated(xc, conv_w, window_strides=(1,), padding=((K - 1, K - 1),), feature_group_count=Idim)
            xc = xc[:, :, :L] + conv_b[None, :, None]
            u = jax.nn.silu(jnp.swapaxes(xc, 1, 2))
            ssm_in = u @ x_proj_w
            dt_in, Bc, Cc = jnp.split(ssm_in, [R, R + N], axis=-1)
            dt = jax.nn.softplus(dt_in @ dt_proj_w + dt_proj_b)
            A = -jnp.exp(A_log)

            def step(state, xs):
                dt_t, B_t, C_t, u_t = xs
                dA = jnp.exp(dt_t[:, :, None] * A[None])
                state = state * dA + (dt_t * u_t)[:, :, None] * B_t[:, None, :]
                y_t = jnp.einsum('bin,bn->bi', state, C_t)
                return (state, y_t)
            xs = (jnp.swapaxes(dt, 0, 1), jnp.swapaxes(Bc, 0, 1), jnp.swapaxes(Cc, 0, 1), jnp.swapaxes(u, 0, 1))
            state0 = jnp.zeros((Bsz, Idim, N), dt.dtype)
            _, ys = jax.lax.scan(step, state0, xs)
            y = jnp.swapaxes(ys, 0, 1)
            y = (y + u * D) * jax.nn.silu(gate)
            return y @ out_proj_w
        return _mamba_forward(input_states, in_proj_w, conv_w, conv_b, x_proj_w, dt_proj_w, dt_proj_b, A_log, D, out_proj_w)

    def _L0_xattn_ref(B, T, C, w, u, k, v):
        import jax, jax.numpy as jnp
        import numpy as np
        B_DIM, T_DIM, C_DIM = (16, 128, 256)

        def _wkv(w, u, k, v):
            Bn, Tn, Cn = k.shape
            NEG_INF = jnp.float32(-1e+38)

            def step(carry, kv_t):
                p, q, o = carry
                kt, vt = kv_t
                no = jnp.maximum(o, u + kt)
                A = jnp.exp(o - no)
                E = jnp.exp(u + kt - no)
                y = (A * p + E * vt) / (A * q + E)
                no2 = jnp.maximum(w + o, kt)
                A2 = jnp.exp(w + o - no2)
                E2 = jnp.exp(kt - no2)
                return ((A2 * p + E2 * vt, A2 * q + E2, no2), y)
            init = (jnp.zeros((Bn, Cn), k.dtype), jnp.zeros((Bn, Cn), k.dtype), jnp.full((Bn, Cn), NEG_INF, k.dtype))
            kT = jnp.moveaxis(k, 1, 0)
            vT = jnp.moveaxis(v, 1, 0)
            _, yT = jax.lax.scan(step, init, (kT, vT))
            return jnp.moveaxis(yT, 0, 1)
        return _wkv(w, u, k, v)

    def _L0_ffn_ref(x, weight, bias):
        import jax, jax.numpy as jnp
        import numpy as np
        B, S, D_IN, D_OUT = (4, 256, 256, 256)
        EPS = 1e-10
        scale = jnp.mean(jnp.abs(weight))
        w_t = jnp.clip(jnp.round(weight / (scale + EPS)), -1.0, 1.0)
        w_ste = weight + jax.lax.stop_gradient(w_t * scale - weight)
        return jnp.einsum('bsi,oi->bso', x, w_ste) + bias
    x = x + _L0_attn_ref(_layernorm(x, axis=-1), L0_attn_in_proj_w, L0_attn_conv_w, L0_attn_conv_b, L0_attn_x_proj_w, L0_attn_dt_proj_w, L0_attn_dt_proj_b, L0_attn_A_log, L0_attn_D, L0_attn_out_proj_w)
    x = x + _L0_xattn_ref(16, 128, 256, L0_xattn_w, L0_xattn_u, _layernorm(x, axis=-1), ctx_2048)
    x = x + _L0_ffn_ref(_layernorm(x, axis=-1), L0_ffn_weight, L0_ffn_bias)
    return x

_drawn_inputs = setup_inputs


def setup_inputs(seed=0):
    import zlib

    import numpy as np

    out = dict(_drawn_inputs(seed))
    spreads = {'L0_attn_conv_b': (0.0, 0.1), 'L0_attn_D': (1.0, 0.2)}
    factors = {'L0_attn_dt_proj_b': 2.707, 'L0_ffn_bias': 3.938}
    for name, (base, spread) in spreads.items():
        noise = np.random.default_rng([zlib.crc32(name.encode()), seed]).standard_normal(out[name].shape)
        drawn = base * np.exp(spread * noise) if base else spread * noise
        out[name] = jnp.asarray(drawn.astype(out[name].dtype))
    for name, factor in factors.items():
        out[name] = (out[name] * factor).astype(out[name].dtype)
    return out
```

```python
from contextlib import ExitStack

from concourse import mybir
from concourse.alu_op_type import AluOpType as ALU

F32 = mybir.dt.float32
ACT = mybir.ActivationFunctionType
AX_X = mybir.AxisListType.X

P = 128
LN_EPS = 1e-5
TERNARY_EPS = 1e-10
ROUND_MAGIC = 12582912.0
NEG_INF = -1e38
VEC_LOADS = 8
INIT_STEPS = 10
TERN_STEPS = 9


def build_decoder(nc, x, ctxT, in_proj_w, conv_w, conv_b, x_proj_w, dt_proj_w, dt_proj_b, A_log, D_skip,
                  out_proj_w, wkv_w, wkv_u, ffn_wT, ffn_b, out):
    BATCH, T, HID = x.shape
    INTER, NSTATE = A_log.shape
    RANK = dt_proj_w.shape[0]
    KCONV = conv_w.shape[2]
    assert T == P and RANK == P
    NB = 4
    GROUPS = BATCH // NB
    TOK = NB * T
    MT = INTER // P
    CT = HID // P
    SLOTS = NSTATE * MT
    PAD = KCONV - 1
    STATE_RING, C_RING = 4, 4
    LN_VAR, LN_STEPS = 2 * NB + 1, 2 * NB + 5

    FRONT_TILES, BACK_TILES = 22, 10
    F_XNT, F_HID, F_GATE, F_DTIN, F_BC, F_BT, F_DT, F_DTUT = 0, 2, 6, 10, 11, 12, 14, 18
    B_OUT, B_KT, B_YT, B_X3T, B_FFN = 0, 2, 4, 6, 8
    PER_ITER = FRONT_TILES + BACK_TILES

    def front_tile(g, k):
        base = (0, 0) if isinstance(g, int) and g == 0 else (PER_ITER * g - BACK_TILES, PER_ITER // 2 * g - BACK_TILES // 2)
        return base[0] + k, k % 2, base[1] + k // 2

    def back_tile(g, k):
        if isinstance(g, int) and g == GROUPS - 1:
            number = GROUPS * FRONT_TILES + (GROUPS - 1) * BACK_TILES
            return number + k, k % 2, number // 2 + k // 2
        return PER_ITER * g + 2 * FRONT_TILES + k, k % 2, PER_ITER // 2 * g + FRONT_TILES + k // 2

    with ExitStack() as ctx:
        def sb(name, shape):
            return ctx.enter_context(nc.sbuf_tensor(name, shape, F32))

        def sem(name):
            return ctx.enter_context(nc.semaphore(name))

        def wait(eng, s, count):
            if not (isinstance(count, int) and count <= 0):
                eng.wait_ge(s, count)

        ident = sb("ident", [P, P])
        w_in = sb("w_in", [P, CT, 2 * INTER])
        w_x = sb("w_x", [P, MT, RANK + 2 * NSTATE])
        w_dt = sb("w_dt", [P, INTER])
        w_out = sb("w_out", [P, MT, HID])
        w_ffnT = sb("w_ffnT", [P, CT, HID])
        ffn_bias = sb("ffn_bias", [P, HID])
        taps = sb("taps", [P, MT, KCONV])
        conv_bias = sb("conv_bias", [P, MT])
        dt_bias = sb("dt_bias", [P, MT])
        skip = sb("skip", [P, MT])
        A_neg = sb("A_neg", [P, MT, NSTATE])
        decay_w = sb("decay_w", [P, CT])
        bonus_u = sb("bonus_u", [P, CT])
        decay_row = sb("decay_row", [P, CT, NB, T])
        small = sb("small", [P, 4])

        xin = sb("xin", [P, NB, HID])
        stats = [sb("stats_f", [P, NB, 6]), sb("stats_b", [P, NB, 6])]
        meanvar = [sb("meanvar_f", [P, NB, 2]), sb("meanvar_b", [P, NB, 2])]
        rstd = [sb("rstd_f", [P, 4, NB]), sb("rstd_b", [P, 4, NB])]
        xn = sb("xn", [P, NB, HID])
        xnT = sb("xnT", [P, CT, TOK])
        hidden = sb("hidden", [P, MT, NB, PAD + T])
        conv = sb("conv", [P, MT, TOK])
        u = sb("u", [P, 2, MT, TOK])
        gate = sb("gate", [P, 2, MT, TOK])
        bcT = sb("bcT", [P, TOK])
        b_col = sb("b_col", [P, 2, NB, NSTATE])
        sp_log = sb("sp_log", [P, MT, TOK])
        dt = sb("dt", [P, MT, NB, T])
        dtuT = sb("dtuT", [P, NB, INTER])

        decay = sb("decay", [P, 2, MT, NB, T])
        inT = sb("inT", [P, 2, NB, INTER])
        state = sb("state", [P, STATE_RING, MT, TOK])
        c_rep = sb("c_rep", [P, C_RING, TOK])

        x2 = sb("x2", [P, NB, HID])
        onew = sb("onew", [P, CT * TOK])[:, :]
        vT = sb("vT", [P, CT * TOK])
        oprev = sb("oprev", [P, CT * NB, T])
        pbuf = sb("pbuf", [P, 1 + CT * TOK])
        qbuf = sb("qbuf", [P, 1 + CT * TOK])

        sp_lin = conv
        dtu = sp_log
        dt_in = xn[:, 0:2, :].rearrange("p b c -> p (b c)")
        z = conv
        ex_upd = sp_log[:, :, :].rearrange("p (h c) t -> p h (c t)", h=2)
        ex_out = conv[:, :, :].rearrange("p (h c) t -> p h (c t)", h=2)
        x3T = xnT
        outb = vT[:, :].rearrange("p (b c) -> p b c", b=NB)
        w_ffn = x2[:, 0:CT, :]
        ones = vT[:, 0:P]

        def dead_gate(gp, half):
            return gate[:, gp, CT * half:CT * half + CT, :].rearrange("p c t -> p (c t)")

        def dead_u(gp, half):
            return u[:, gp, CT * half:CT * half + CT, :].rearrange("p c t -> p (c t)")

        psY = ctx.enter_context(nc.psum_tensor("psY", [P, MT, TOK], F32))
        psR = ctx.enter_context(nc.psum_tensor("psR", [P, 2, TOK], F32))
        psM = ctx.enter_context(nc.psum_tensor("psM", [P, 2, TOK], F32))

        c_dram = nc.dram_tensor("c_rows", (GROUPS, NSTATE, TOK), F32, kind="Internal").ap()

        ld = {k: sem("ld_" + k) for k in ("vec", "w_in", "w_x", "w_dt", "w_out", "w_ffn")}
        ld_x, ld_x2, ld_ctx, ld_c = sem("ld_x"), sem("ld_x2"), sem("ld_ctx"), [sem(f"ld_c{i}") for i in range(C_RING)]
        c_stored, out_stored = sem("c_stored"), sem("out_stored")
        pool_init, dve_init, a_init = sem("pool_init"), sem("dve_init"), sem("a_init")
        tern_dve, tern_pe = sem("tern_dve"), sem("tern_pe")
        tile_done = sem("tile_done")
        bank_read = [sem("bank_read0"), sem("bank_read1")]
        ln_dve, ln_act = [sem("ln_dve_f"), sem("ln_dve_b")], [sem("ln_act_f"), sem("ln_act_b")]
        xn_ok = [sem("xn_f_ok"), sem("xn_b_ok")]
        conv_ok, u_ok, sp_exp, sp_ln, dt_ok, dtu_ok = (sem("conv_ok"), sem("u_ok"), sem("sp_exp"), sem("sp_ln"),
                                                       sem("dt_ok"), sem("dtu_ok"))
        decay_ok, inT_ok, ring_ok, scan_ok, prod_ok, sum_ok = (sem("decay_ok"), sem("inT_ok"), sem("ring_ok"),
                                                              sem("scan_ok"), sem("prod_ok"), sem("sum_ok"))
        skip_ok, z_ok, omax_ok, oprev_ok = sem("skip_ok"), sem("z_ok"), sem("omax_ok"), sem("oprev_ok")
        upd_arg, upd_exp, out_arg, out_exp = sem("upd_arg"), sem("upd_exp"), sem("out_arg"), sem("out_exp")
        ev_upd_ok, ev_out_ok, p_ok, q_ok = sem("ev_upd_ok"), sem("ev_out_ok"), sem("p_ok"), sem("q_ok")
        den_ok, rec_ok, num_ok, y_ok = sem("den_ok"), sem("rec_ok"), sem("num_ok"), sem("y_ok")
        x3b_ok = sem("x3b_ok")

        x_g = x.rearrange("(g b) t c -> g t b c", b=NB)
        ctx_g = ctxT.rearrange("(c p) (g t) -> g p c t", p=P, g=GROUPS)
        out_g = out.rearrange("(g b) t c -> g t b c", b=NB)

        def tile_read(eng, tile):
            _, bank, turn = tile
            eng.wait_ge(bank_read[bank], turn + 1)

        PE_BACK = {5: [0], 6: [1], 11: [2], 12: [3], 27: [4], 28: [5], 33: [6], 34: [7], 37: [8], 38: [9]}
        PE_FRONT = {39: [0], 40: [1], 41: [2], 42: [3], 43: [4], 44: [5], 45: [6], 46: [7], 47: [8], 48: [9],
                    50: [10], 51: [11], 53: [12], 54: [13], 55: [14], 56: [15], 57: [16], 58: [17],
                    63: [18, 19, 20, 21]}
        ACT_BACK = {11: [0], 15: [1], 16: [2], 19: [3], 23: [4], 25: [5], 28: [6], 35: [7], 38: [8], 39: [9]}
        ACT_FRONT = {40: [0], 43: [1], 44: [2], 45: [3], 46: [4], 47: [5], 48: [6], 49: [7], 50: [8], 51: [9],
                     52: [10, 11], 53: [12], 58: [13], 59: [14], 60: [15], 61: [16, 17], 63: [18, 19, 20, 21]}
        DVE_BACK = {0: [0], 6: [1], 7: [2], 8: [3], 10: [4], 14: [5], 16: [6], 18: [7], 21: [8], 22: [9], 24: [10],
                    26: [11], 28: [12], 29: [13], 30: [14], 32: [15], 38: [16], 39: [17]}
        DVE_FRONT = {35: [0], 37: [1], 43: [2], 45: [3], 51: [4], 52: [5], 54: [6], 55: [7], 60: [8]}
        POOL_BACK = {0: [0], 4: [1], 5: [2], 7: [3]}
        POOL_FRONT = {14: [0]}
        SP_BACK = {9: [1]}
        SP_FRONT = {5: [0], 12: [1]}

        def pieces(table, at, piece, g):
            for k in table.get(at, []):
                piece(g, k)

        block = ctx.enter_context(nc.Block())

        @block.sync
        def _(sp):
            def front_piece(g, k):
                if k == 0:
                    wait(sp, xn_ok[0], NB * g)
                    sp.dma_start(xin[:, :, :], x_g[g]).then_inc(ld_x, 16)
                else:
                    tile_read(sp, front_tile(g, F_BC))
                    sp.dma_start(c_dram[g], bcT[NSTATE:2 * NSTATE, :]).then_inc(c_stored, 16)

            def back_piece(g, k):
                if k == 0:
                    if isinstance(g, int) and g == 0:
                        sp.wait_ge(tern_dve, TERN_STEPS)
                    else:
                        tile_read(sp, back_tile(g - 1, B_FFN + 1))
                    sp.dma_start(x2[:, :, :], x_g[g]).then_inc(ld_x2, 16)
                    wait(sp, out_stored, 2 * 16 * g)
                    sp.dma_start(vT[:, :].rearrange("p (c t) -> p c t", c=CT), ctx_g[g]).then_inc(ld_ctx, 16)
                else:
                    for h in range(2):
                        tile_read(sp, back_tile(g, B_FFN + h))
                        sp.dma_start(out_g[g][:, 2 * h:2 * h + 2], outb[:, 2 * h:2 * h + 2]).then_inc(out_stored, 16)

            def broadcast_c(g, n):
                wait(sp, prod_ok, NSTATE * g + n - C_RING + 1)
                if n == 0:
                    sp.wait_ge(c_stored, 16 * (g + 1))
                sp.dma_start(c_rep[:, n % C_RING, :], c_dram[g, n:n + 1, :].broadcast_to((P, TOK))).then_inc(ld_c[n % C_RING], 16)

            front_piece(0, 0)
            sp.dma_start(w_in[:, :, :], in_proj_w.rearrange("(k p) n -> p k n", p=P)).then_inc(ld["w_in"], 16)
            sp.dma_start(taps[:, :, :], conv_w.rearrange("(m p) a k -> p m (a k)", p=P)).then_inc(ld["vec"], 16)
            for dst, src in ((conv_bias, conv_b), (dt_bias, dt_proj_b), (skip, D_skip), (decay_w, wkv_w), (bonus_u, wkv_u)):
                sp.dma_start(dst[:, :], src).then_inc(ld["vec"], 16)
            sp.dma_start(A_neg[:, :, :], A_log.rearrange("(m p) n -> p m n", p=P)).then_inc(ld["vec"], 16)
            sp.dma_start(ffn_bias[:, :], ffn_b.rearrange("(a n) -> a n", a=1).broadcast_to((P, HID))).then_inc(ld["vec"], 16)
            sp.dma_start(w_x[:, :, :], x_proj_w.rearrange("(m p) n -> p m n", p=P)).then_inc(ld["w_x"], 16)
            sp.dma_start(w_dt[:, :], dt_proj_w).then_inc(ld["w_dt"], 16)
            sp.dma_start(w_ffn, ffn_wT.rearrange("(c p) o -> p c o", p=P)).then_inc(ld["w_ffn"], 16)
            sp.dma_start(w_out[:, :, :], out_proj_w.rearrange("(m p) n -> p m n", p=P)).then_inc(ld["w_out"], 16)
            front_piece(0, 1)

            def iteration(g, back, front):
                for n in range(NSTATE):
                    broadcast_c(g, n)
                    if back and n == 0:
                        back_piece(g - 1, 0)
                    if back:
                        pieces(SP_BACK, n, back_piece, g - 1)
                    if front:
                        pieces(SP_FRONT, n, front_piece, g + 1)

            iteration(0, False, True)
            for g in range(1, GROUPS - 1):
                iteration(g, True, True)
            iteration(GROUPS - 1, True, False)
            back_piece(GROUPS - 1, 0)
            back_piece(GROUPS - 1, 1)
            sp.wait_ge(out_stored, 2 * 16 * GROUPS)

        @block.tensor
        def _(pe):
            def open_tile(tile):
                _, bank, turn = tile
                wait(pe, bank_read[bank], turn)
                return psM[:, bank, :]

            def transpose4(ps, src):
                for i in range(4):
                    last = nc.tensor.transpose(ps[:, i * P:(i + 1) * P], src(i), ident[:, :])
                return last

            def project(ps, lhs, rhs, ksteps):
                for k in range(ksteps):
                    last = nc.tensor.matmul(ps, lhs(k), rhs(k), start=(k == 0), stop=(k == ksteps - 1))
                return last

            def front_piece(g, k):
                first = isinstance(g, int) and g == 0
                gp = g % 2
                ps = open_tile(front_tile(g, k))
                if k < F_HID:
                    pe.wait_ge(xn_ok[0], NB * (g + 1))
                    last = transpose4(ps, lambda b: xn[:, b, k * P:(k + 1) * P])
                elif k < F_DTIN:
                    if k == F_HID:
                        tile_read(pe, front_tile(g, F_XNT))
                        tile_read(pe, front_tile(g, F_XNT + 1))
                        if first:
                            pe.wait_ge(ld["w_in"], 16)
                    j = k - F_HID
                    last = project(ps, lambda c: w_in[:, c, j * P:(j + 1) * P], lambda c: xnT[:, c, :], CT)
                elif k == F_DTIN:
                    pe.wait_ge(u_ok, MT * (g + 1))
                    if first:
                        pe.wait_ge(ld["w_x"], 16)
                    last = project(ps, lambda m: w_x[:, m, 0:RANK], lambda m: u[:, gp, m, :], MT)
                elif k == F_BC:
                    last = project(ps[0:2 * NSTATE, :], lambda m: w_x[:, m, RANK:RANK + 2 * NSTATE],
                                   lambda m: u[:, gp, m, :], MT)
                elif k < F_DT:
                    tile_read(pe, front_tile(g, F_BC))
                    for i in range(2):
                        b = 2 * (k - F_BT) + i
                        last = nc.tensor.transpose(ps[:, i * NSTATE:(i + 1) * NSTATE], bcT[0:NSTATE, b * T:(b + 1) * T],
                                                   ident[0:NSTATE, 0:NSTATE])
                elif k < F_DTUT:
                    tile_read(pe, front_tile(g, F_DTIN))
                    if first:
                        pe.wait_ge(ld["w_dt"], 16)
                    m = k - F_DT
                    last = project(ps, lambda _: w_dt[:, m * P:(m + 1) * P], lambda _: dt_in, 1)
                else:
                    pe.wait_ge(dtu_ok, g + 1)
                    b = k - F_DTUT
                    last = transpose4(ps, lambda m: dtu[:, m, b * T:(b + 1) * T])
                last.then_inc(tile_done, 1)

            def back_piece(g, k):
                ps = open_tile(back_tile(g, k))
                if k < B_KT:
                    pe.wait_ge(z_ok, g + 1)
                    if isinstance(g, int) and g == 0:
                        pe.wait_ge(ld["w_out"], 16)
                    for i in range(2):
                        b = 2 * (k - B_OUT) + i
                        last = project(ps[:, i * HID:(i + 1) * HID], lambda m: z[:, m, b * T:(b + 1) * T],
                                       lambda m: w_out[:, m, :], MT)
                elif k < B_YT or B_X3T <= k < B_FFN:
                    second = k >= B_X3T
                    c = k - (B_X3T if second else B_KT)
                    pe.wait_ge(xn_ok[1], NB * (2 * g + 1 + second))
                    last = transpose4(ps, lambda b: xn[:, b, c * P:(c + 1) * P])
                elif k < B_X3T:
                    pe.wait_ge(y_ok, 3 * (g + 1))
                    h = k - B_YT
                    last = transpose4(ps, lambda i: onew[:, (i % 2) * TOK + (2 * h + i // 2) * T:
                                                         (i % 2) * TOK + (2 * h + i // 2 + 1) * T])
                else:
                    tile_read(pe, back_tile(g, B_X3T))
                    tile_read(pe, back_tile(g, B_X3T + 1))
                    for i in range(2):
                        b = 2 * (k - B_FFN) + i
                        last = project(ps[:, i * HID:(i + 1) * HID], lambda c: x3T[:, c, b * T:(b + 1) * T],
                                       lambda c: w_ffnT[:, c, :], CT)
                last.then_inc(tile_done, 1)

            def scan_input(g, n, m):
                if m == 0:
                    pe.wait_ge(inT_ok, NB * (NSTATE * g + n + 1))
                wait(pe, scan_ok, SLOTS * g + MT * n + m - 1)
                transpose4(psR[:, m % 2, :], lambda b: inT[:, n % 2, b, m * P:(m + 1) * P]).then_inc(ring_ok, 1)

            def sum_states(g, n, m):
                if m == 0:
                    pe.wait_ge(prod_ok, NSTATE * g + n + 1)
                if n == 0:
                    wait(pe, skip_ok, MT * (g - 1) + m + 1)
                last = nc.tensor.matmul(psY[:, m, :], ident[:, :], state[:, n % STATE_RING, m, :],
                                        start=(n == 0), stop=(n == NSTATE - 1))
                if m == MT - 1:
                    last.then_inc(sum_ok, 1)

            pe.wait_ge(pool_init, 2)
            for k in range(FRONT_TILES):
                front_piece(0, k)
            pe.wait_ge(tern_dve, 1)
            pe.wait_ge(dve_init, 1)
            nc.tensor.matmul(psY[:, 0, 0:P], ones, small[:, 0:1].broadcast_to((P, P)), start=True, stop=True).then_inc(tern_pe, 1)
            pe.wait_ge(tern_dve, TERN_STEPS)

            def iteration(g, back, front):
                for n in range(NSTATE):
                    for m in range(MT):
                        scan_input(g, n, m)
                        if n >= 2:
                            sum_states(g, n - 2, m)
                        if back:
                            pieces(PE_BACK, MT * n + m, back_piece, g - 1)
                        if front:
                            pieces(PE_FRONT, MT * n + m, front_piece, g + 1)
                for n in (NSTATE - 2, NSTATE - 1):
                    for m in range(MT):
                        sum_states(g, n, m)

            iteration(0, False, True)
            for g in range(1, GROUPS - 1):
                iteration(g, True, True)
            iteration(GROUPS - 1, True, False)
            for k in range(BACK_TILES):
                back_piece(GROUPS - 1, k)

        @block.scalar
        def _(act):
            def evacuate(out_ap, tile, func=ACT.Copy, view=lambda ps: ps):
                number, bank, _ = tile
                act.wait_ge(tile_done, number + 1)
                nc.scalar.activation(out_ap, view(psM[:, bank, :]), func).then_inc(bank_read[bank], 1)

            def inv_std(part, nth):
                rs = rstd[part]
                act.wait_ge(ln_dve[part], LN_STEPS * nth + LN_VAR)
                nc.scalar.activation(rs[:, 1, :], rs[:, 0, :], ACT.Ln).then_inc(ln_act[part], 1)
                act.wait_ge(ln_act[part], 2 * nth + 1)
                nc.scalar.activation(rs[:, 1, :], rs[:, 1, :], ACT.Exp, scale=-0.5).then_inc(ln_act[part], 1)

            def front_piece(g, k):
                gp = g % 2
                if k == 0:
                    inv_std(0, g)
                elif k < 3:
                    evacuate(xnT[:, k - 1, :], front_tile(g, F_XNT + k - 1))
                elif k < 7:
                    evacuate(hidden[:, k - 3, :, PAD:], front_tile(g, F_HID + k - 3),
                             view=lambda ps: ps.rearrange("p (b t) -> p b t", b=NB))
                elif k < 11:
                    m = k - 7
                    if m == 0 and not (isinstance(g, int) and g < 2):
                        tile_read(act, back_tile(g - 2, B_FFN + 1))
                    evacuate(gate[:, gp, m, :], front_tile(g, F_GATE + m), ACT.Silu)
                elif k < 13:
                    for m in (2 * (k - 11), 2 * (k - 11) + 1):
                        act.wait_ge(conv_ok, MT * KCONV * g + 2 * KCONV * (m // 2) + 2 * (KCONV - 1) + m % 2 + 1)
                        nc.scalar.activation(u[:, gp, m, :], conv[:, m, :], ACT.Silu,
                                             bias=conv_bias[:, m:m + 1]).then_inc(u_ok, 1)
                elif k < 17:
                    m = k - 13
                    number, bank, _ = front_tile(g, F_DT + m)
                    act.wait_ge(tile_done, number + 1)
                    nc.scalar.activation(sp_lin[:, m, :], psM[:, bank, :], ACT.Relu, bias=dt_bias[:, m:m + 1])
                    nc.scalar.activation(sp_log[:, m, :], psM[:, bank, :], ACT.Abs,
                                         bias=dt_bias[:, m:m + 1]).then_inc(bank_read[bank], 1)
                elif k == 17:
                    for m in (MT - 2, MT - 1):
                        tile_read(act, front_tile(g, F_DT + m))
                    nc.scalar.activation(sp_log[:, :, :], sp_log[:, :, :], ACT.Exp, scale=-1.0).then_inc(sp_exp, 1)
                    act.wait_ge(sp_exp, g + 1)
                    nc.scalar.activation(sp_log[:, :, :], sp_log[:, :, :], ACT.Ln, bias=1.0).then_inc(sp_ln, 1)
                else:
                    b = k - 18
                    evacuate(dtuT[:, b, :], front_tile(g, F_DTUT + b))

            def back_piece(g, k):
                gp = g % 2
                if k == 0:
                    inv_std(1, 2 * g)
                elif k < 3:
                    evacuate(dead_gate(gp, 0)[:, (k - 1) * TOK:k * TOK], back_tile(g, B_KT + k - 1))
                elif k == 3:
                    act.wait_ge(omax_ok, g + 1)
                    nc.scalar.activation(oprev[:, :, 1:T], dead_u(gp, 0).rearrange("p (s t) -> p s t", t=T)[:, :, 0:T - 1],
                                         ACT.Copy).then_inc(oprev_ok, 1)
                elif k == 4:
                    act.wait_ge(upd_arg, 3 * (g + 1))
                    nc.scalar.activation(ex_upd, ex_upd, ACT.Exp).then_inc(upd_exp, 1)
                elif k == 5:
                    act.wait_ge(out_arg, 5 * (g + 1))
                    nc.scalar.activation(ex_out, ex_out, ACT.Exp).then_inc(out_exp, 1)
                elif k == 6:
                    act.wait_ge(den_ok, 2 * (g + 1))
                    act.wait_ge(p_ok, g + 1)
                    act.wait_ge(q_ok, g + 1)
                    nc.scalar.activation(ex_upd[:, 0], dead_u(gp, 0), ACT.Ln).then_inc(rec_ok, 1)
                    act.wait_ge(rec_ok, 2 * g + 1)
                    nc.scalar.activation(ex_upd[:, 0], ex_upd[:, 0], ACT.Exp, scale=-1.0).then_inc(rec_ok, 1)
                elif k == 7:
                    inv_std(1, 2 * g + 1)
                else:
                    evacuate(x3T[:, k - 8, :], back_tile(g, B_X3T + k - 8))

            def decay_step(g, n, m):
                if m == 0:
                    if n == 0:
                        act.wait_ge(dt_ok, g + 1)
                    wait(act, scan_ok, MT * (NSTATE * g + n - 1))
                nc.scalar.activation(decay[:, n % 2, m, :, 1:T], dt[:, m, :, 1:T], ACT.Exp,
                                     scale=A_neg[:, m, n:n + 1]).then_inc(decay_ok, 1)

            def input_step(g, n, b):
                if b == 0:
                    if n == 0:
                        for i in range(2):
                            tile_read(act, front_tile(g, F_BT + i))
                            tile_read(act, front_tile(g, F_DTUT + 2 + i))
                    wait(act, ring_ok, MT * (NSTATE * g + n - 1))
                nc.scalar.activation(inT[:, n % 2, b, :], dtuT[:, b, :], ACT.Copy,
                                     scale=b_col[:, g % 2, b, n:n + 1]).then_inc(inT_ok, 1)

            act.wait_ge(ld["vec"], VEC_LOADS * 16)
            nc.scalar.activation(A_neg[:, :, :], A_neg[:, :, :], ACT.Exp).then_inc(a_init, 1)
            act.wait_ge(a_init, 1)
            nc.scalar.activation(A_neg[:, :, :], A_neg[:, :, :], ACT.Copy, scale=-1.0).then_inc(a_init, 1)
            act.wait_ge(a_init, 2)
            for k in range(22):
                front_piece(0, k)
            act.wait_ge(dve_init, INIT_STEPS)

            def iteration(g, back, front):
                for n in range(NSTATE):
                    for m in range(MT):
                        input_step(g, n, m)
                        decay_step(g, n, m)
                        if back:
                            pieces(ACT_BACK, MT * n + m, back_piece, g - 1)
                        if front:
                            pieces(ACT_FRONT, MT * n + m, front_piece, g + 1)

            iteration(0, False, True)
            for g in range(1, GROUPS - 1):
                iteration(g, True, True)
            iteration(GROUPS - 1, True, False)
            for k in range(10):
                back_piece(GROUPS - 1, k)

        @block.vector
        def _(dve):
            def read_tile(tile):
                number, bank, _ = tile
                dve.wait_ge(tile_done, number + 1)
                return psM[:, bank, :], bank_read[bank]

            def variances(part, nth, src):
                st, mv, done = stats[part], meanvar[part], LN_STEPS * nth
                for b in range(NB):
                    nc.vector.bn_stats(st[:, b, :], src[:, b, :]).then_inc(ln_dve[part], 1)
                for b in range(NB):
                    dve.wait_ge(ln_dve[part], done + b + 1)
                    nc.vector.bn_aggr(mv[:, b, :], st[:, b, :]).then_inc(ln_dve[part], 1)
                dve.wait_ge(ln_dve[part], done + 2 * NB)
                nc.vector.tensor_scalar(rstd[part][:, 0, :], mv[:, :, 1], LN_EPS, None, ALU.add).then_inc(ln_dve[part], 1)

            def normalise(part, nth, src):
                rs, mv, done = rstd[part], meanvar[part], LN_STEPS * nth + LN_VAR
                v, r, t, r1 = rs[:, 0, :], rs[:, 1, :], rs[:, 2, :], rs[:, 3, :]
                dve.wait_ge(ln_act[part], 2 * (nth + 1))
                nc.vector.tensor_tensor(t, r, r, ALU.mult).then_inc(ln_dve[part], 1)
                dve.wait_ge(ln_dve[part], done + 1)
                nc.vector.tensor_tensor(t, t, v, ALU.mult).then_inc(ln_dve[part], 1)
                dve.wait_ge(ln_dve[part], done + 2)
                nc.vector.tensor_scalar(t, t, -0.5, 1.5, ALU.mult, ALU.add).then_inc(ln_dve[part], 1)
                dve.wait_ge(ln_dve[part], done + 3)
                nc.vector.tensor_tensor(r1, r, t, ALU.mult).then_inc(ln_dve[part], 1)
                dve.wait_ge(ln_dve[part], done + 4)
                for b in range(NB):
                    nc.vector.tensor_scalar(xn[:, b, :], src[:, b, :], mv[:, b, 0:1], rs[:, 3, b:b + 1],
                                            ALU.subtract, ALU.mult).then_inc(xn_ok[part], 1)

            def front_piece(g, k):
                gp = g % 2
                if k == 0:
                    dve.wait_ge(ld_x, 16 * (g + 1))
                    variances(0, g, xin)
                elif k == 1:
                    if not (isinstance(g, int) and g < 2):
                        dve.wait_ge(tile_done, back_tile(g - 2, B_X3T + 1)[0] + 1)
                    normalise(0, g, xin)
                elif k < 4:
                    ms = (2 * (k - 2), 2 * (k - 2) + 1)
                    done = MT * KCONV * g + 2 * KCONV * (k - 2)
                    for j in range(KCONV):
                        for i, m in enumerate(ms):
                            src, acc = hidden[:, m, :, j:j + T], conv[:, m, :].rearrange("p (b t) -> p b t", b=NB)
                            if j == 0:
                                tile_read(dve, front_tile(g, F_HID + m))
                                op = nc.vector.tensor_scalar(acc, src, taps[:, m, 0:1], None, ALU.mult)
                            else:
                                dve.wait_ge(conv_ok, done + 2 * (j - 1) + i + 1)
                                op = nc.vector.scalar_tensor_tensor(acc, src, taps[:, m, j:j + 1], acc, ALU.mult, ALU.add)
                            op.then_inc(conv_ok, 1)
                elif k == 4:
                    ps, read = read_tile(front_tile(g, F_DTIN))
                    nc.vector.tensor_copy(dt_in, ps).then_inc(read, 1)
                elif k == 5:
                    wait(dve, c_stored, 16 * g)
                    ps, read = read_tile(front_tile(g, F_BC))
                    nc.vector.tensor_copy(bcT[0:2 * NSTATE, :], ps[0:2 * NSTATE, :]).then_inc(read, 1)
                elif k < 8:
                    ps, read = read_tile(front_tile(g, F_BT + k - 6))
                    nc.vector.tensor_copy(b_col[:, gp, 2 * (k - 6):2 * (k - 6) + 2, :].rearrange("p b n -> p (b n)"),
                                          ps[:, 0:2 * NSTATE]).then_inc(read, 1)
                else:
                    dve.wait_ge(sp_ln, g + 1)
                    wait(dve, decay_ok, SLOTS * g)
                    nc.vector.tensor_tensor(dt[:, :, :, :].rearrange("p m b t -> p m (b t)"), sp_lin[:, :, :],
                                            sp_log[:, :, :], ALU.add).then_inc(dt_ok, 1)

            def back_piece(g, k):
                gp = g % 2
                kT, omax, ev_upd, ev_out = dead_gate(gp, 0), dead_u(gp, 0), dead_u(gp, 1), dead_gate(gp, 1)
                prev = oprev[:, :, :].rearrange("p s t -> p (s t)")
                halves = [slice(c * TOK, (c + 1) * TOK) for c in range(CT)]
                if k == 0:
                    dve.wait_ge(sum_ok, NSTATE * (g + 1))
                    for m in range(MT):
                        nc.vector.scalar_tensor_tensor(z[:, m, :], u[:, gp, m, :], skip[:, m:m + 1], psY[:, m, :],
                                                       ALU.mult, ALU.add).then_inc(skip_ok, 1)
                elif k < 3:
                    h = slice(2 * (k - 1), 2 * k)
                    if k == 1:
                        dve.wait_ge(ld_x2, 16 * (g + 1))
                    ps, read = read_tile(back_tile(g, B_OUT + k - 1))
                    nc.vector.tensor_tensor(x2[:, h, :], x2[:, h, :], ps.rearrange("p (b c) -> p b c", b=2), ALU.add).then_inc(read, 1)
                elif k == 3:
                    for i in range(2):
                        tile_read(dve, back_tile(g, B_OUT + i))
                    variances(1, 2 * g, x2)
                elif k == 4:
                    normalise(1, 2 * g, x2)
                elif k == 5:
                    for i in range(CT):
                        tile_read(dve, back_tile(g, B_KT + i))
                    nc.vector.tensor_tensor_scan(omax, decay_row[:, :, :, :].rearrange("p c b t -> p (c b t)"), kT, 0.0,
                                                 ALU.add, ALU.max).then_inc(omax_ok, 1)
                elif k == 6:
                    dve.wait_ge(omax_ok, g + 1)
                    nc.vector.tensor_tensor(ex_upd[:, 1], kT, omax, ALU.subtract).then_inc(upd_arg, 1)
                    dve.wait_ge(oprev_ok, g + 1)
                    for c, h in enumerate(halves):
                        nc.vector.scalar_tensor_tensor(ex_upd[:, 0, h], prev[:, h], decay_w[:, c:c + 1], omax[:, h],
                                                       ALU.add, ALU.subtract).then_inc(upd_arg, 1)
                elif k == 7:
                    for c, h in enumerate(halves):
                        nc.vector.scalar_tensor_tensor(onew[:, h], kT[:, h], bonus_u[:, c:c + 1], prev[:, h],
                                                       ALU.add, ALU.max).then_inc(out_arg, 1)
                    for c, h in enumerate(halves):
                        dve.wait_ge(out_arg, 5 * g + c + 1)
                        nc.vector.scalar_tensor_tensor(ex_out[:, 1, h], kT[:, h], bonus_u[:, c:c + 1], onew[:, h],
                                                       ALU.add, ALU.subtract).then_inc(out_arg, 1)
                    nc.vector.tensor_tensor(ex_out[:, 0], prev, onew, ALU.subtract).then_inc(out_arg, 1)
                elif k == 8:
                    dve.wait_ge(upd_exp, g + 1)
                    nc.vector.tensor_tensor_scan(qbuf[:, 1:], ex_upd[:, 0], ex_upd[:, 1], 0.0, ALU.mult, ALU.add).then_inc(q_ok, 1)
                elif k == 9:
                    dve.wait_ge(ev_upd_ok, g + 1)
                    nc.vector.tensor_tensor_scan(pbuf[:, 1:], ex_upd[:, 0], ev_upd, 0.0, ALU.mult, ALU.add).then_inc(p_ok, 1)
                elif k == 10:
                    den, num = omax, kT
                    dve.wait_ge(out_exp, g + 1)
                    dve.wait_ge(q_ok, g + 1)
                    nc.vector.tensor_tensor(den, ex_out[:, 0], qbuf[:, 0:CT * TOK], ALU.mult).then_inc(den_ok, 1)
                    dve.wait_ge(p_ok, g + 1)
                    nc.vector.tensor_tensor(num, ex_out[:, 0], pbuf[:, 0:CT * TOK], ALU.mult).then_inc(num_ok, 1)
                    dve.wait_ge(den_ok, 2 * g + 1)
                    nc.vector.tensor_tensor(den, den, ex_out[:, 1], ALU.add).then_inc(den_ok, 1)
                    dve.wait_ge(ev_out_ok, g + 1)
                    dve.wait_ge(num_ok, 2 * g + 1)
                    nc.vector.tensor_tensor(num, num, ev_out, ALU.add).then_inc(num_ok, 1)
                elif k == 11:
                    den, num, r = omax, kT, ex_upd[:, 0]
                    dve.wait_ge(rec_ok, 2 * (g + 1))
                    nc.vector.tensor_tensor(den, den, r, ALU.mult).then_inc(y_ok, 1)
                    dve.wait_ge(num_ok, 2 * (g + 1))
                    nc.vector.tensor_tensor(num, num, r, ALU.mult).then_inc(y_ok, 1)
                    dve.wait_ge(y_ok, 3 * g + 2)
                    nc.vector.scalar_tensor_tensor(onew, den, 2.0, num, ALU.subtract, ALU.mult).then_inc(y_ok, 1)
                elif k < 14:
                    h = slice(2 * (k - 12), 2 * (k - 12) + 2)
                    ps, read = read_tile(back_tile(g, B_YT + k - 12))
                    nc.vector.tensor_tensor(x2[:, h, :], x2[:, h, :], ps.rearrange("p (b c) -> p b c", b=2),
                                            ALU.subtract).then_inc(read, 1)
                elif k == 14:
                    for i in range(2):
                        tile_read(dve, back_tile(g, B_YT + i))
                    variances(1, 2 * g + 1, x2)
                elif k == 15:
                    normalise(1, 2 * g + 1, x2)
                else:
                    h = slice(2 * (k - 16), 2 * (k - 16) + 2)
                    x3b = dead_gate(gp, 0).rearrange("p (b c) -> p b c", b=NB)
                    dve.wait_ge(x3b_ok, g + 1)
                    ps, read = read_tile(back_tile(g, B_FFN + k - 16))
                    nc.vector.tensor_tensor(outb[:, h, :], x3b[:, h, :], ps.rearrange("p (b c) -> p b c", b=2), ALU.add).then_inc(read, 1)

            def scan_step(g, n, m):
                slot = SLOTS * g + MT * n + m
                if m == 0:
                    wait(dve, sum_ok, NSTATE * g + n - STATE_RING + 1)
                dve.wait_ge(decay_ok, slot + 1)
                dve.wait_ge(ring_ok, slot + 1)
                nc.vector.tensor_tensor_scan(state[:, n % STATE_RING, m, :], decay[:, n % 2, m].rearrange("p b t -> p (b t)"),
                                             psR[:, m % 2, :], 0.0, ALU.mult, ALU.add).then_inc(scan_ok, 1)

            nc.vector.memset(ones, 1.0).then_inc(dve_init, 1)
            nc.vector.memset(hidden[:, :, :, 0:PAD].rearrange("p m b k -> p (m b) k"), 0.0).then_inc(dve_init, 1)
            nc.vector.memset(decay[:, :, :, :, 0:1].rearrange("p a m b o -> p (a m b) o"), 0.0).then_inc(dve_init, 1)
            nc.vector.memset(oprev[:, :, 0:1], NEG_INF).then_inc(dve_init, 1)
            nc.vector.memset(pbuf[:, 0:1], 0.0).then_inc(dve_init, 1)
            nc.vector.memset(qbuf[:, 0:1], 0.0).then_inc(dve_init, 1)
            nc.vector.memset(decay_row[:, :, :, :], 0.0).then_inc(dve_init, 1)
            dve.wait_ge(ld["vec"], VEC_LOADS * 16)
            dve.wait_ge(dve_init, 7)
            for c in range(CT):
                nc.vector.tensor_scalar(decay_row[:, c], decay_row[:, c], decay_w[:, c:c + 1], None, ALU.add).then_inc(dve_init, 1)
            dve.wait_ge(dve_init, 7 + CT)
            nc.vector.memset(decay_row[:, :, :, 0:1].rearrange("p c b o -> p (c b) o"), NEG_INF).then_inc(dve_init, 1)
            dve.wait_ge(dve_init, INIT_STEPS)
            for k in range(9):
                front_piece(0, k)
            dve.wait_ge(ld["w_ffn"], 16)
            nc.vector.tensor_reduce(small[:, 0:1], w_ffn.rearrange("p o i -> p (o i)"), AX_X, ALU.add,
                                    apply_absolute_value=True).then_inc(tern_dve, 1)
            dve.wait_ge(tern_pe, 1)
            nc.vector.tensor_scalar(small[:, 1:2], psY[:, 0, 0:1], 1.0 / (HID * HID), None, ALU.mult).then_inc(tern_dve, 1)
            dve.wait_ge(tern_dve, 2)
            nc.vector.tensor_scalar(small[:, 2:3], small[:, 1:2], TERNARY_EPS, None, ALU.add).then_inc(tern_dve, 1)
            dve.wait_ge(tern_dve, 3)
            nc.vector.reciprocal(small[:, 3:4], small[:, 2:3]).then_inc(tern_dve, 1)
            dve.wait_ge(tern_dve, 4)
            nc.vector.tensor_scalar(w_ffnT[:, :, :], w_ffn, small[:, 3:4], 1.0, ALU.mult, ALU.min).then_inc(tern_dve, 1)
            dve.wait_ge(tern_dve, 5)
            nc.vector.tensor_scalar(w_ffnT[:, :, :], w_ffnT[:, :, :], -1.0, ROUND_MAGIC, ALU.max, ALU.add).then_inc(tern_dve, 1)
            dve.wait_ge(tern_dve, 6)
            nc.vector.tensor_scalar(w_ffnT[:, :, :], w_ffnT[:, :, :], ROUND_MAGIC, small[:, 1:2], ALU.subtract, ALU.mult).then_inc(tern_dve, 1)
            dve.wait_ge(tern_dve, 7)
            nc.vector.tensor_tensor(w_ffnT[:, :, :], w_ffnT[:, :, :], w_ffn, ALU.subtract).then_inc(tern_dve, 1)
            dve.wait_ge(tern_dve, 8)
            nc.vector.tensor_tensor(w_ffnT[:, :, :], w_ffnT[:, :, :], w_ffn, ALU.add).then_inc(tern_dve, 1)

            def iteration(g, back, front):
                for n in range(NSTATE):
                    for m in range(MT):
                        scan_step(g, n, m)
                        if back:
                            pieces(DVE_BACK, MT * n + m, back_piece, g - 1)
                        if front:
                            pieces(DVE_FRONT, MT * n + m, front_piece, g + 1)

            iteration(0, False, True)
            for g in range(1, GROUPS - 1):
                iteration(g, True, True)
            iteration(GROUPS - 1, True, False)
            for k in range(18):
                back_piece(GROUPS - 1, k)

        @block.gpsimd
        def _(pool):
            def front_piece(g, _):
                pool.wait_ge(dt_ok, g + 1)
                pool.wait_ge(u_ok, MT * (g + 1))
                nc.gpsimd.tensor_tensor(dtu[:, :, :], dt[:, :, :, :].rearrange("p m b t -> p m (b t)"), u[:, g % 2],
                                        ALU.mult).then_inc(dtu_ok, 1)

            def back_piece(g, k):
                gp = g % 2
                if k == 0:
                    pool.wait_ge(skip_ok, MT * (g + 1))
                    nc.gpsimd.tensor_tensor(z[:, :, :], z[:, :, :], gate[:, gp], ALU.mult).then_inc(z_ok, 1)
                elif k == 1:
                    pool.wait_ge(upd_exp, g + 1)
                    pool.wait_ge(ld_ctx, 16 * (g + 1))
                    nc.gpsimd.tensor_tensor(dead_u(gp, 1), ex_upd[:, 1], vT[:, :], ALU.mult).then_inc(ev_upd_ok, 1)
                elif k == 2:
                    pool.wait_ge(out_exp, g + 1)
                    nc.gpsimd.tensor_tensor(dead_gate(gp, 1), ex_out[:, 1], vT[:, :], ALU.mult).then_inc(ev_out_ok, 1)
                else:
                    for i in range(2):
                        tile_read(pool, back_tile(g, B_YT + i))
                    nc.gpsimd.tensor_tensor(dead_gate(gp, 0).rearrange("p (b c) -> p b c", b=NB), x2[:, :, :],
                                            ffn_bias[:, :].rearrange("p (o c) -> p o c", o=1).broadcast_to((P, NB, HID)),
                                            ALU.add).then_inc(x3b_ok, 1)

            def product_step(g, n):
                pool.wait_ge(scan_ok, MT * (NSTATE * g + n + 1))
                pool.wait_ge(ld_c[n % C_RING], 16 * (NSTATE // C_RING * g + n // C_RING + 1))
                s = state[:, n % STATE_RING]
                nc.gpsimd.tensor_tensor(s, s, c_rep[:, n % C_RING:n % C_RING + 1, :].broadcast_to((P, MT, TOK)),
                                        ALU.mult).then_inc(prod_ok, 1)

            nc.gpsimd.memset(ident[:, :], 0.0).then_inc(pool_init, 1)
            pool.wait_ge(pool_init, 1)
            nc.gpsimd.affine_select(out=ident[:, :], in_=ident[:, :], compare_op=ALU.not_equal, fill=1.0, base=0,
                                    pattern=[[-1, P]], channel_multiplier=1).then_inc(pool_init, 1)
            front_piece(0, 0)

            def iteration(g, back, front):
                for n in range(NSTATE):
                    product_step(g, n)
                    if back:
                        pieces(POOL_BACK, n, back_piece, g - 1)
                    if front:
                        pieces(POOL_FRONT, n, front_piece, g + 1)

            iteration(0, False, True)
            for g in range(1, GROUPS - 1):
                iteration(g, True, True)
            iteration(GROUPS - 1, True, False)
            for k in range(4):
                back_piece(GROUPS - 1, k)


_INS = ["x", "ctx_2048", "L0_attn_in_proj_w", "L0_attn_conv_w", "L0_attn_conv_b", "L0_attn_x_proj_w",
        "L0_attn_dt_proj_w", "L0_attn_dt_proj_b", "L0_attn_A_log", "L0_attn_D", "L0_attn_out_proj_w",
        "L0_xattn_w", "L0_xattn_u", "L0_ffn_weight", "L0_ffn_bias"]

_VECTORS = ["L0_attn_conv_b", "L0_attn_dt_proj_b", "L0_attn_D", "L0_xattn_w", "L0_xattn_u"]


def kernel(**inputs):
    import numpy as np
    from concourse import bacc
    from concourse.bass_utils import run_bass_kernel_spmd

    nc = bacc.Bacc("TRN2", target_bir_lowering=False, num_devices=1)
    arrays, args = {}, []
    for name in _INS:
        a = np.asarray(inputs[name])
        if name == "ctx_2048":
            a = a.transpose(2, 0, 1).reshape(a.shape[2], -1)
        elif name == "L0_ffn_weight":
            a = a.T
        elif name in _VECTORS:
            a = a.reshape(-1, P).T
        a = np.ascontiguousarray(a)
        arrays[f"in_{name}"] = a
        args.append(nc.dram_tensor(f"in_{name}", a.shape, mybir.dt.from_np(a.dtype), kind="ExternalInput").ap())
    shape = tuple(inputs["x"].shape)
    args.append(nc.dram_tensor("out_0", shape, F32, kind="ExternalOutput").ap())
    build_decoder(nc, *args)
    r = run_bass_kernel_spmd(nc, [arrays], core_ids=[0])
    return r.results[0]["out_0"]
```

```python
from contextlib import ExitStack

from concourse import mybir
from concourse.alu_op_type import AluOpType as ALU

F32 = mybir.dt.float32
I32 = mybir.dt.int32
ACT = mybir.ActivationFunctionType
AX_X = mybir.AxisListType.X

P = 128
LN_EPS = 1e-5
TERNARY_EPS = 1e-10
ROUND_MAGIC = 12582912.0
NEG_INF = -1e38
RSQRT_GUESS = float(0x5F3759DF)
NEWTON = 3
VEC_LOADS = 8
INIT_STEPS = 7
TERN_STEPS = 9


def build_decoder(nc, x, ctxT, in_proj_w, conv_w, conv_b, x_proj_w, dt_proj_w, dt_proj_b, A_log, D_skip,
                  out_proj_w, wkv_w, wkv_u, ffn_wT, ffn_b, out):
    BATCH, T, HID = x.shape
    INTER, NSTATE = A_log.shape
    RANK = dt_proj_w.shape[0]
    KCONV = conv_w.shape[2]
    assert T == P and RANK == P
    NB = 4
    GROUPS = BATCH // NB
    TOK = NB * T
    MT = INTER // P
    CT = HID // P
    SLOTS = NSTATE * MT
    STATE_RING, C_RING = 4, 4
    PAIRED = ()
    PAIRS, SUMS = len(PAIRED), NSTATE - len(PAIRED)
    PRODS = NSTATE - 1 + MT

    def prods_to(n):
        return n + 1 if n < NSTATE - 1 else PRODS

    def pairs_to(n):
        return sum(k <= n for k in PAIRED)

    def sums_to(n):
        return n + 1 - sum(k <= n + 1 for k in PAIRED)

    def sums_due(n):
        return [k for k in (n - 3, n - 2) if 0 <= k < NSTATE and k + 1 not in PAIRED and (k == n - 3) == (k in PAIRED)]

    HB = NB // 2
    HT = HB * T
    LN_VAR, LN_STEPS = 2 * HB + 1, 2 * HB + 3 + 3 * NEWTON

    FRONT_TILES, BACK_TILES = 22, 10
    F_XNT, F_HID, F_GATE, F_DTIN, F_DT, F_BC, F_BT, F_DTUT = 0, 2, 6, 10, 11, 15, 16, 18
    B_OUT, B_KT, B_YT, B_X3T, B_FFN = 0, 2, 4, 6, 8
    RING, FRONT_BANK, BACK_BANK = MT, MT + 2, MT + 3
    FIRST_BANKS = (FRONT_BANK, 0, 1, 2, 3, BACK_BANK)
    LAST_BANKS = (BACK_BANK, FRONT_BANK, 0, 1, 2, 3)

    def first_turns(bank):
        return len(range(FIRST_BANKS.index(bank), FRONT_TILES, len(FIRST_BANKS)))

    def front_tile(g, k):
        if isinstance(g, int) and g == 0:
            return FIRST_BANKS[k % len(FIRST_BANKS)], k // len(FIRST_BANKS)
        return FRONT_BANK, FRONT_TILES * g + (first_turns(FRONT_BANK) - FRONT_TILES + k)

    def back_tile(g, k):
        if isinstance(g, int) and g == GROUPS - 1:
            bank, before = LAST_BANKS[k % len(LAST_BANKS)], k // len(LAST_BANKS)
            before += {BACK_BANK: BACK_TILES * g, FRONT_BANK: FRONT_TILES * (GROUPS - 1)}.get(bank, 0)
            return bank, first_turns(bank) + before
        return BACK_BANK, BACK_TILES * g + (first_turns(BACK_BANK) + k)

    with ExitStack() as ctx:
        def sb(name, shape):
            return ctx.enter_context(nc.sbuf_tensor(name, shape, F32))

        def sem(name):
            return ctx.enter_context(nc.semaphore(name))

        def wait(eng, s, count):
            if not (isinstance(count, int) and count <= 0):
                eng.wait_ge(s, count)

        ident = sb("ident", [P, P])
        w_in = sb("w_in", [P, CT, 2 * INTER])
        w_x = sb("w_x", [P, MT, RANK + 2 * NSTATE])
        w_dt = sb("w_dt", [P, INTER])
        w_out = sb("w_out", [P, MT, HID])
        w_ffnT = sb("w_ffnT", [P, CT, HID])
        ffn_bias = sb("ffn_bias", [P, HID])
        taps = sb("taps", [P, MT, KCONV])
        conv_bias = sb("conv_bias", [P, MT])
        dt_bias = sb("dt_bias", [P, MT])
        skip = sb("skip", [P, MT])
        A_neg = sb("A_neg", [P, MT, NSTATE])
        decay_w = sb("decay_w", [P, CT])
        bonus_u = sb("bonus_u", [P, CT])
        decay_row = sb("decay_row", [P, CT, NB, T])
        small = sb("small", [P, 4])

        xin = sb("xin", [P, NB, HID])
        stats = [sb("stats_f", [P, NB, 6]), sb("stats_b", [P, NB, 6])]
        meanvar = [sb("meanvar_f", [P, NB, 2]), sb("meanvar_b", [P, NB, 2])]
        rstd = [sb("rstd_f", [P, 3, NB]), sb("rstd_b", [P, 3, NB])]
        xn = [sb("xn_f", [P, NB, HID]), sb("xn_b", [P, NB, HID])]
        xnT = sb("xnT", [P, CT, TOK])
        room_hpq = sb("room_hpq", [P, 2 * (1 + CT * TOK)])
        conv = sb("conv", [P, MT, TOK])
        u = sb("u", [P, 2, MT, TOK])
        gate = sb("gate", [P, 2, MT, TOK])
        bcT = sb("bcT", [P, TOK])
        b_col = sb("b_col", [P, 2, NB, NSTATE])
        sp_log = sb("sp_log", [P, MT, TOK])
        dt = sb("dt", [P, MT, NB, T])
        dtuT = sb("dtuT", [P, NB, INTER])

        decay = sb("decay", [P, 2, MT, NB, T])
        inT = sb("inT", [P, 2, NB, INTER])
        state = sb("state", [P, STATE_RING, MT, TOK])
        c_rep = sb("c_rep", [P, C_RING, TOK])

        x2 = sb("x2", [P, NB, HID])
        onew = sb("onew", [P, CT * TOK])[:, :]
        vT = sb("vT", [P, CT * TOK])
        x3T = sb("x3T", [P, CT, TOK])
        oprev = sb("oprev", [P, CT * NB, T])

        hidden = room_hpq[:, 0:MT * TOK].rearrange("p (m b t) -> p m b t", m=MT, b=NB)
        pq = room_hpq[:, :].rearrange("p (a s) -> p a s", a=2)
        pbuf, qbuf = pq[:, 0, :], pq[:, 1, :]
        sp_lin = conv
        dtu = sp_log
        dt_in = xn[0][:, 0:2, :].rearrange("p b c -> p (b c)")
        z = conv
        ex_upd = sp_log[:, :, :].rearrange("p (h c) t -> p h (c t)", h=2)
        ex_out = conv[:, :, :].rearrange("p (h c) t -> p h (c t)", h=2)
        outb = vT[:, :].rearrange("p (b c) -> p b c", b=NB)
        w_ffn = x2[:, 0:CT, :]
        ones = vT[:, 0:P]

        def dead_gate(gp, half):
            return gate[:, gp, CT * half:CT * half + CT, :].rearrange("p c t -> p (c t)")

        def dead_u(gp, half):
            return u[:, gp, CT * half:CT * half + CT, :].rearrange("p c t -> p (c t)")

        psum = ctx.enter_context(nc.psum_tensor("psum", [P, MT + 4, TOK], F32))
        psY, psR = psum[:, 0:MT], psum[:, RING:RING + 2]

        c_dram = nc.dram_tensor("c_rows", (GROUPS, NSTATE, TOK), F32, kind="Internal").ap()

        ld = {k: sem("ld_" + k) for k in ("vec", "w_in", "w_x", "w_dt", "w_out", "w_ffn")}
        ld_x, ld_x2, ld_ctx, ld_c = [sem("ld_x0"), sem("ld_x1")], sem("ld_x2"), sem("ld_ctx"), [sem(f"ld_c{i}") for i in range(C_RING)]
        c_stored, room_v_free = sem("c_stored"), sem("room_v_free")
        pool_init, dve_init, a_init = sem("pool_init"), sem("dve_init"), sem("a_init")
        tern_dve, tern_pe = sem("tern_dve"), sem("tern_pe")
        bank_done = {b: sem(f"bank{b}_done") for b in FIRST_BANKS}
        bank_read = {b: sem(f"bank{b}_read") for b in FIRST_BANKS}
        ln_dve = [sem("ln_dve_f"), sem("ln_dve_b")]
        xn_ok = [sem("xn_f_ok"), sem("xn_b_ok")]
        conv_ok, u_ok, sp_exp, sp_ln, dt_ok, dtu_ok, dt_new = (sem("conv_ok"), sem("u_ok"), sem("sp_exp"), sem("sp_ln"),
                                                       sem("dt_ok"), sem("dtu_ok"), sem("dt_new"))
        decay_ok, inT_ok, ring_ok, scan_ok, prod_ok, sum_ok = (sem("decay_ok"), sem("inT_ok"), sem("ring_ok"),
                                                              sem("scan_ok"), sem("prod_ok"), sem("sum_ok"))
        pair_ok = sem("pair_ok")
        skip_ok, z_ok, omax_ok, oprev_ok = sem("skip_ok"), sem("z_ok"), sem("omax_ok"), sem("oprev_ok")
        upd_arg, upd_exp, out_arg, out_exp = sem("upd_arg"), sem("upd_exp"), sem("out_arg"), sem("out_exp")
        ev_upd_ok, ev_out_ok, p_ok, q_ok = sem("ev_upd_ok"), sem("ev_out_ok"), sem("p_ok"), sem("q_ok")
        den_ok, rec_ok, num_ok, y_ok = sem("den_ok"), sem("rec_ok"), sem("num_ok"), sem("y_ok")
        x3b_ok, pq_zero = sem("x3b_ok"), sem("pq_zero")

        x_g = x.rearrange("(g b) t c -> g t b c", b=NB)
        ctx_g = ctxT.rearrange("(c p) (g t) -> g p c t", p=P, g=GROUPS)
        out_g = out.rearrange("(g b) t c -> g t b c", b=NB)

        def tile_done(eng, tile):
            bank, turn = tile
            eng.wait_ge(bank_done[bank], turn + 1)

        def tile_read(eng, tile):
            bank, turn = tile
            eng.wait_ge(bank_read[bank], turn + 1)

        PE_BACK = {7: [0], 8: [1], 15: [2, 3], 30: [4], 33: [5], 34: [6], 36: [7, 8], 39: [9]}
        PE_FRONT = {38: [0], 39: [1], 41: [2], 42: [3], 43: [4], 44: [5, 6], 46: [7, 8], 47: [9], 49: [10], 50: [11], 52: [12], 53: [13], 54: [14], 56: [15], 57: [16], 58: [17], 60: [18], 61: [19], 62: [20], 63: [21]}
        ACT_BACK = {21: [0], 25: [1], 26: [2], 31: [3]}
        ACT_FRONT = {52: [0], 62: [1], 63: [2, 3, 4, 5]}
        DVE_BACK = {4: [0], 5: [1], 7: [2], 8: [3, 4], 9: [5], 10: [6], 12: [7], 14: [8], 15: [9], 16: [10], 18: [11], 21: [12], 23: [13, 14], 26: [15], 28: [16], 30: [17, 18], 31: [19], 32: [20, 21], 33: [22], 35: [23], 36: [24], 38: [25], 43: [26]}
        DVE_FRONT = {22: [0, 1], 36: [2, 3], 38: [4], 40: [5], 41: [6], 42: [7], 43: [8, 9, 10], 45: [11, 12], 46: [13, 14], 47: [15, 16, 17], 49: [18, 19], 52: [20], 53: [21], 54: [22], 55: [23], 58: [24, 25], 59: [26], 60: [27]}
        POOL_BACK = {0: [0], 1: [1], 4: [2], 5: [3], 8: [4]}
        POOL_FRONT = {13: [0, 1]}
        SP_BACK = {10: [1]}
        SP_FRONT = {4: [0], 15: [1]}

        def pieces(table, at, piece, g):
            for k in table.get(at, []):
                piece(g, k)

        def hold_wait(eng):
            eng.nop(nofuse=True)

        block = ctx.enter_context(nc.Block())

        @block.sync
        def _(sp):
            def front_piece(g, k):
                if k == 0:
                    wait(sp, xn_ok[0], NB * g)
                    for h in range(2):
                        sp.dma_start(xin[:, HB * h:HB * h + HB, :], x_g[g][:, HB * h:HB * h + HB]).then_inc(ld_x[h], 16)
                else:
                    tile_read(sp, front_tile(g, F_BC))
                    sp.dma_start(c_dram[g], bcT[NSTATE:2 * NSTATE, :]).then_inc(c_stored, 16)

            def back_piece(g, k):
                if k == 0:
                    sp.wait_ge(tern_dve, TERN_STEPS)
                    if not (isinstance(g, int) and g == 0):
                        tile_read(sp, back_tile(g - 1, B_FFN + 1))
                    sp.dma_start(x2[:, :, :], x_g[g]).then_inc(ld_x2, 16)
                    sp.wait_ge(room_v_free, 2 * 16 * g + 1)
                    sp.dma_start(vT[:, :].rearrange("p (c t) -> p c t", c=CT), ctx_g[g]).then_inc(ld_ctx, 16)
                else:
                    for h in range(2):
                        tile_read(sp, back_tile(g, B_FFN + h))
                        sp.dma_start(out_g[g][:, 2 * h:2 * h + 2], outb[:, 2 * h:2 * h + 2]).then_inc(room_v_free, 16)

            def broadcast_c(g, n):
                lap, old = divmod(n - C_RING, NSTATE)
                wait(sp, prod_ok, PRODS * g + PRODS * lap + prods_to(old))
                if n == 0:
                    sp.wait_ge(c_stored, 16 * (g + 1))
                sp.dma_start(c_rep[:, n % C_RING, :], c_dram[g, n:n + 1, :].broadcast_to((P, TOK))).then_inc(ld_c[n % C_RING], 16)

            front_piece(0, 0)
            sp.dma_start(w_in[:, :, :], in_proj_w.rearrange("(k p) n -> p k n", p=P)).then_inc(ld["w_in"], 16)
            sp.dma_start(taps[:, :, :], conv_w.rearrange("(m p) a k -> p m (a k)", p=P)).then_inc(ld["vec"], 16)
            for dst, src in ((conv_bias, conv_b), (dt_bias, dt_proj_b), (skip, D_skip), (decay_w, wkv_w), (bonus_u, wkv_u)):
                sp.dma_start(dst[:, :], src).then_inc(ld["vec"], 16)
            sp.dma_start(A_neg[:, :, :], A_log.rearrange("(m p) n -> p m n", p=P)).then_inc(ld["vec"], 16)
            sp.dma_start(ffn_bias[:, :], ffn_b.rearrange("(a n) -> a n", a=1).broadcast_to((P, HID))).then_inc(ld["vec"], 16)
            sp.dma_start(w_x[:, :, :], x_proj_w.rearrange("(m p) n -> p m n", p=P)).then_inc(ld["w_x"], 16)
            sp.dma_start(w_dt[:, :], dt_proj_w).then_inc(ld["w_dt"], 16)
            sp.dma_start(w_ffn, ffn_wT.rearrange("(c p) o -> p c o", p=P)).then_inc(ld["w_ffn"], 16)
            sp.dma_start(w_out[:, :, :], out_proj_w.rearrange("(m p) n -> p m n", p=P)).then_inc(ld["w_out"], 16)
            front_piece(0, 1)

            def iteration(g, back, front):
                for n in range(NSTATE):
                    broadcast_c(g, n)
                    if back and n == 0:
                        back_piece(g - 1, 0)
                    if back:
                        pieces(SP_BACK, n, back_piece, g - 1)
                    if front:
                        pieces(SP_FRONT, n, front_piece, g + 1)

            iteration(0, False, True)
            with sp.Fori(1, GROUPS - 1) as g:
                iteration(g, True, True)
            iteration(GROUPS - 1, True, False)
            back_piece(GROUPS - 1, 0)
            back_piece(GROUPS - 1, 1)
            sp.wait_ge(room_v_free, 2 * 16 * GROUPS + 1)

        @block.tensor
        def _(pe):
            def open_tile(tile):
                bank, turn = tile
                wait(pe, bank_read[bank], turn)
                return psum[:, bank, :]

            def input_read(tile):
                if isinstance(tile[1], int):
                    tile_read(pe, tile)

            def transpose4(ps, src):
                for i in range(4):
                    last = nc.tensor.transpose(ps[:, i * P:(i + 1) * P], src(i), ident[:, :])
                return last

            def project(ps, lhs, rhs, ksteps):
                for k in range(ksteps):
                    last = nc.tensor.matmul(ps, lhs(k), rhs(k), start=(k == 0), stop=(k == ksteps - 1))
                return last

            def front_piece(g, k):
                first = isinstance(g, int) and g == 0
                gp = g % 2
                ps = open_tile(front_tile(g, k))
                if k < F_HID:
                    pe.wait_ge(xn_ok[0], NB * g + HB * (k + 1))
                    last = transpose4(ps, lambda i: xn[0][:, HB * k + i % HB, (i // HB) * P:(i // HB + 1) * P])
                elif k < F_DTIN:
                    if k == F_HID:
                        input_read(front_tile(g, F_XNT + 1))
                        if first:
                            pe.wait_ge(ld["w_in"], 16)
                    j = k - F_HID
                    last = project(ps, lambda c: w_in[:, c, j * P:(j + 1) * P], lambda c: xnT[:, c, :], CT)
                elif k == F_DTIN:
                    if first:
                        pe.wait_ge(ld["w_x"], 16)
                    for m in range(MT):
                        if first or m == 0:
                            pe.wait_ge(u_ok, MT * g + (m + 1 if first else MT))
                        last = nc.tensor.matmul(ps, w_x[:, m, 0:RANK], u[:, gp, m, :], start=(m == 0), stop=(m == MT - 1))
                elif k < F_BC:
                    input_read(front_tile(g, F_DTIN))
                    if first:
                        pe.wait_ge(ld["w_dt"], 16)
                    m = k - F_DT
                    last = project(ps, lambda _: w_dt[:, m * P:(m + 1) * P], lambda _: dt_in, 1)
                elif k == F_BC:
                    hold_wait(pe)
                    last = project(ps[0:2 * NSTATE, :], lambda m: w_x[:, m, RANK:RANK + 2 * NSTATE],
                                   lambda m: u[:, gp, m, :], MT)
                elif k < F_DTUT:
                    input_read(front_tile(g, F_BC))
                    hold_wait(pe)
                    for i in range(2):
                        b = 2 * (k - F_BT) + i
                        last = nc.tensor.transpose(ps[:, i * NSTATE:(i + 1) * NSTATE], bcT[0:NSTATE, b * T:(b + 1) * T],
                                                   ident[0:NSTATE, 0:NSTATE])
                else:
                    b = k - F_DTUT
                    pe.wait_ge(dtu_ok, 2 * g + b // HB + 1)
                    last = transpose4(ps, lambda m: dtu[:, m, b * T:(b + 1) * T])
                last.then_inc(bank_done[front_tile(g, k)[0]], 1)

            def back_piece(g, k):
                ps = open_tile(back_tile(g, k))
                if k < B_KT:
                    pe.wait_ge(z_ok, 2 * g + k - B_OUT + 1)
                    pe.wait_ge(ld["w_out"], 16)
                    for i in range(2):
                        b = 2 * (k - B_OUT) + i
                        last = project(ps[:, i * HID:(i + 1) * HID], lambda m: z[:, m, b * T:(b + 1) * T],
                                       lambda m: w_out[:, m, :], MT)
                elif k < B_YT:
                    c = k - B_KT
                    pe.wait_ge(xn_ok[1], NB * (2 * g + 1))
                    last = transpose4(ps, lambda b: xn[1][:, b, c * P:(c + 1) * P])
                elif B_X3T <= k < B_FFN:
                    h = k - B_X3T
                    pe.wait_ge(xn_ok[1], NB * (2 * g + 1) + HB * (h + 1))
                    last = transpose4(ps, lambda i: xn[1][:, HB * h + i % HB, (i // HB) * P:(i // HB + 1) * P])
                elif k < B_X3T:
                    pe.wait_ge(y_ok, 3 * (g + 1))
                    h = k - B_YT
                    last = transpose4(ps, lambda i: onew[:, (i % 2) * TOK + (2 * h + i // 2) * T:
                                                         (i % 2) * TOK + (2 * h + i // 2 + 1) * T])
                else:
                    input_read(back_tile(g, B_X3T + k - B_FFN))
                    for i in range(2):
                        b = 2 * (k - B_FFN) + i
                        last = project(ps[:, i * HID:(i + 1) * HID], lambda c: x3T[:, c, b * T:(b + 1) * T],
                                       lambda c: w_ffnT[:, c, :], CT)
                last.then_inc(bank_done[back_tile(g, k)[0]], 1)

            def scan_input(g, n, m):
                if m == 0:
                    pe.wait_ge(inT_ok, NB * (NSTATE * g + n + 1))
                wait(pe, scan_ok, SLOTS * g + MT * n + m - 1)
                transpose4(psR[:, m % 2, :], lambda b: inT[:, n % 2, b, m * P:(m + 1) * P]).then_inc(ring_ok, 1)

            def sum_states(g, n, m):
                if m == 0 and n in PAIRED:
                    pe.wait_ge(pair_ok, PAIRS * g + pairs_to(n))
                elif m == 0 or n == NSTATE - 1:
                    pe.wait_ge(prod_ok, PRODS * g + n + m + 1)
                if n == 0:
                    if isinstance(g, int) and g == 0:
                        pe.wait_ge(bank_read[m], first_turns(m))
                    else:
                        pe.wait_ge(skip_ok, 2 * MT * g - MT + m + 1)
                last = nc.tensor.matmul(psY[:, m, :], ident[:, :], state[:, n % STATE_RING, m, :],
                                        start=(n == 0), stop=(n == NSTATE - 1))
                if m == MT - 1:
                    last.then_inc(sum_ok, 1)

            pe.wait_ge(pool_init, 2)
            for k in range(F_DTIN):
                front_piece(0, k)
            pe.wait_ge(tern_dve, 1)
            pe.wait_ge(dve_init, 1)
            nc.tensor.matmul(psR[:, 0, 0:P], ones, small[:, 0:1].broadcast_to((P, P)), start=True, stop=True).then_inc(tern_pe, 1)
            for k in range(F_DTIN, FRONT_TILES):
                front_piece(0, k)
            pe.wait_ge(tern_dve, 2)
            pe.nop(nofuse=True).then_inc(room_v_free, 1)

            def iteration(g, back, front):
                for n in range(NSTATE):
                    for m in range(MT):
                        scan_input(g, n, m)
                        for k in sums_due(n):
                            sum_states(g, k, m)
                        if back:
                            pieces(PE_BACK, MT * n + m, back_piece, g - 1)
                        if front:
                            pieces(PE_FRONT, MT * n + m, front_piece, g + 1)
                for n in sums_due(NSTATE) + sums_due(NSTATE + 1) + sums_due(NSTATE + 2):
                    for m in range(MT):
                        sum_states(g, n, m)

            iteration(0, False, True)
            with pe.Fori(1, GROUPS - 1) as g:
                iteration(g, True, True)
            iteration(GROUPS - 1, True, False)
            for k in range(BACK_TILES):
                back_piece(GROUPS - 1, k)

        @block.scalar
        def _(act):
            def evacuate(out_ap, tile, view=lambda ps: ps):
                bank, _ = tile
                tile_done(act, tile)
                nc.scalar.activation(out_ap, view(psum[:, bank, :]), ACT.Copy).then_inc(bank_read[bank], 1)

            def front_piece(g, k):
                gp = g % 2
                if k == 0:
                    if isinstance(g, int) and g == 0:
                        for m in range(MT):
                            silu_tile(m)
                    for m in range(MT):
                        act.wait_ge(conv_ok, MT * KCONV * g + 2 * KCONV * (m // 2) + 2 * (KCONV - 1) + m % 2 + 1)
                        nc.scalar.activation(u[:, gp, m, :], conv[:, m, :], ACT.Silu,
                                             bias=conv_bias[:, m:m + 1]).then_inc(u_ok, 1)
                    if not (isinstance(g, int) and g == 0):
                        tile_read(act, front_tile(g, F_GATE + MT - 1))
                        nc.scalar.activation(gate[:, gp], gate[:, gp], ACT.Silu)
                elif k == 1:
                    tile_read(act, front_tile(g, F_DT + MT - 1))
                    nc.scalar.activation(sp_log[:, :, :], sp_lin[:, :, :], ACT.Abs).then_inc(sp_exp, 1)
                    act.wait_ge(sp_exp, 2 * g + 1)
                    nc.scalar.activation(sp_log[:, :, :], sp_log[:, :, :], ACT.Exp, scale=-1.0).then_inc(sp_exp, 1)
                    act.wait_ge(sp_exp, 2 * g + 2)
                    nc.scalar.activation(sp_log[:, :, :], sp_log[:, :, :], ACT.Ln, bias=1.0).then_inc(sp_ln, 1)
                else:
                    b = k - 2
                    evacuate(dtuT[:, b, :], front_tile(g, F_DTUT + b))

            def silu_tile(m):
                bank, _ = front_tile(0, F_GATE + m)
                tile_done(act, front_tile(0, F_GATE + m))
                nc.scalar.activation(gate[:, 0, m, :], psum[:, bank, :], ACT.Silu).then_inc(bank_read[bank], 1)

            def copy_dt(g):
                act.wait_ge(dt_new, 2 * (g + 1))
                nc.scalar.activation(dt[:, :, :, :].rearrange("p m b t -> p m (b t)"), sp_lin[:, :, :],
                                     ACT.Copy).then_inc(dt_ok, 1)

            def back_piece(g, k):
                gp = g % 2
                if k == 0:
                    act.wait_ge(omax_ok, g + 1)
                    nc.scalar.activation(oprev[:, :, 1:T], dead_u(gp, 0).rearrange("p (s t) -> p s t", t=T)[:, :, 0:T - 1],
                                         ACT.Copy).then_inc(oprev_ok, 1)
                elif k == 1:
                    act.wait_ge(upd_arg, 3 * (g + 1))
                    nc.scalar.activation(ex_upd, ex_upd, ACT.Exp).then_inc(upd_exp, 1)
                elif k == 2:
                    act.wait_ge(out_arg, 5 * (g + 1))
                    nc.scalar.activation(ex_out, ex_out, ACT.Exp).then_inc(out_exp, 1)
                else:
                    act.wait_ge(den_ok, 2 * (g + 1))
                    act.wait_ge(p_ok, g + 1)
                    act.wait_ge(q_ok, g + 1)
                    hold_wait(act)
                    nc.scalar.activation(ex_upd[:, 0], dead_u(gp, 0), ACT.Ln).then_inc(rec_ok, 1)
                    act.wait_ge(rec_ok, 2 * g + 1)
                    nc.scalar.activation(ex_upd[:, 0], ex_upd[:, 0], ACT.Exp, scale=-1.0).then_inc(rec_ok, 1)

            def decay_step(g, n, m):
                src = dt if n else sp_lin[:, :, :].rearrange("p m (b t) -> p m b t", b=NB)
                if n == 0 and m == 0:
                    act.wait_ge(dt_new, 2 * (g + 1))
                if n == 1 and m == 0:
                    act.wait_ge(dt_ok, g + 1)
                if m == 0:
                    wait(act, scan_ok, MT * (NSTATE * g + n - 1))
                nc.scalar.activation(decay[:, n % 2, m, :, 1:T], src[:, m, :, 1:T], ACT.Exp,
                                     scale=A_neg[:, m, n:n + 1]).then_inc(decay_ok, 1)

            def input_step(g, n, b):
                if b == 0:
                    if n == 0:
                        tile_read(act, front_tile(g, F_DTUT + NB - 1))
                    wait(act, ring_ok, MT * (NSTATE * g + n - 1))
                nc.scalar.activation(inT[:, n % 2, b, :], dtuT[:, b, :], ACT.Copy,
                                     scale=b_col[:, g % 2, b, n:n + 1]).then_inc(inT_ok, 1)

            act.wait_ge(ld["vec"], VEC_LOADS * 16)
            nc.scalar.activation(A_neg[:, :, :], A_neg[:, :, :], ACT.Exp).then_inc(a_init, 1)
            act.wait_ge(a_init, 1)
            nc.scalar.activation(A_neg[:, :, :], A_neg[:, :, :], ACT.Copy, scale=-1.0).then_inc(a_init, 1)
            act.wait_ge(a_init, 2)
            for m in range(MT):
                evacuate(hidden[:, m], front_tile(0, F_HID + m), view=lambda ps: ps.rearrange("p (b t) -> p b t", b=NB))
            for k in range(6):
                front_piece(0, k)
            act.wait_ge(dve_init, INIT_STEPS)

            def iteration(g, back, front):
                for n in range(NSTATE):
                    for m in range(MT):
                        if n == 0 and m == 0:
                            for b in range(NB):
                                input_step(g, 0, b)
                        elif n > 0:
                            input_step(g, n, m)
                        decay_step(g, n, m)
                        if n == 0 and m == MT - 1:
                            copy_dt(g)
                        if back:
                            pieces(ACT_BACK, MT * n + m, back_piece, g - 1)
                        if front:
                            pieces(ACT_FRONT, MT * n + m, front_piece, g + 1)

            iteration(0, False, True)
            with act.Fori(1, GROUPS - 1) as g:
                iteration(g, True, True)
            iteration(GROUPS - 1, True, False)
            for k in range(4):
                back_piece(GROUPS - 1, k)

        @block.vector
        def _(dve):
            def read_tile(tile):
                bank, _ = tile
                tile_done(dve, tile)
                return psum[:, bank, :], bank_read[bank]

            def move(out_ap, tile, view=lambda ps: ps):
                ps, read = read_tile(tile)
                nc.vector.tensor_copy(out_ap, view(ps)).then_inc(read, 1)

            def variances(part, nth, h, src):
                st, mv, done = stats[part], meanvar[part], LN_STEPS * nth
                for b in range(HB * h, HB * h + HB):
                    nc.vector.bn_stats(st[:, b, :], src[:, b, :]).then_inc(ln_dve[part], 1)
                dve.wait_ge(ln_dve[part], done + HB)
                hold_wait(dve)
                for b in range(HB * h, HB * h + HB):
                    nc.vector.bn_aggr(mv[:, b, :], st[:, b, :]).then_inc(ln_dve[part], 1)
                dve.wait_ge(ln_dve[part], done + 2 * HB)
                nc.vector.tensor_scalar(rstd[part][:, 0, HB * h:HB * h + HB], mv[:, HB * h:HB * h + HB, 1], LN_EPS, None,
                                        ALU.add).then_inc(ln_dve[part], 1)

            def normalise(part, nth, h, src):
                hs = slice(HB * h, HB * h + HB)
                rs, mv, done = rstd[part], meanvar[part], LN_STEPS * nth + LN_VAR
                v, t, r = rs[:, 0, hs], rs[:, 1, hs], rs[:, 2, hs]
                dve.wait_ge(ln_dve[part], done)
                nc.vector.tensor_scalar(t.bitcast(I32), v.bitcast(I32), 1, None, ALU.logical_shift_right).then_inc(ln_dve[part], 1)
                dve.wait_ge(ln_dve[part], done + 1)
                nc.vector.tensor_scalar(r.bitcast(I32), t.bitcast(I32), -1.0, RSQRT_GUESS, ALU.mult, ALU.add).then_inc(ln_dve[part], 1)
                for i in range(NEWTON):
                    dve.wait_ge(ln_dve[part], done + 3 * i + 2)
                    nc.vector.tensor_tensor(t, r, r, ALU.mult).then_inc(ln_dve[part], 1)
                    dve.wait_ge(ln_dve[part], done + 3 * i + 3)
                    nc.vector.scalar_tensor_tensor(t, t, -0.5, v, ALU.mult, ALU.mult).then_inc(ln_dve[part], 1)
                    dve.wait_ge(ln_dve[part], done + 3 * i + 4)
                    nc.vector.scalar_tensor_tensor(r, t, 1.5, r, ALU.add, ALU.mult).then_inc(ln_dve[part], 1)
                dve.wait_ge(ln_dve[part], done + 3 * NEWTON + 2)
                for b in range(HB * h, HB * h + HB):
                    nc.vector.tensor_scalar(xn[part][:, b, :], src[:, b, :], mv[:, b, 0:1], rs[:, 2, b:b + 1],
                                            ALU.subtract, ALU.mult).then_inc(xn_ok[part], 1)

            def front_piece(g, k):
                gp = g % 2
                if k < 4:
                    h = k // 2
                    if k % 2 == 0:
                        dve.wait_ge(ld_x[h], 16 * (g + 1))
                        variances(0, 2 * g + h, h, xin)
                    else:
                        normalise(0, 2 * g + h, h, xin)
                elif k < 6:
                    h = k - 4
                    move(xnT[:, :, HT * h:HT * h + HT], front_tile(g, F_XNT + h), view=lambda ps: ps.rearrange("p (c t) -> p c t", c=CT))
                elif k < 10:
                    m = k - 6
                    move(hidden[:, m], front_tile(g, F_HID + m), view=lambda ps: ps.rearrange("p (b t) -> p b t", b=NB))
                elif k < 18 and k % 2 == 0:
                    half, first_tap = divmod((k - 10) // 2, 2)
                    ms = (2 * half, 2 * half + 1)
                    done = MT * KCONV * g + 2 * KCONV * half
                    for j in (2 * first_tap, 2 * first_tap + 1):
                        tap = KCONV - 1 - j
                        for i, m in enumerate(ms):
                            acc = conv[:, m, :].rearrange("p (b t) -> p b t", b=NB)[:, :, j:T]
                            src = hidden[:, m, :, 0:T - j]
                            if j == 0:
                                if i == 0:
                                    tile_read(dve, front_tile(g, F_HID + ms[1]))
                                op = nc.vector.tensor_scalar(acc, src, taps[:, m, tap:tap + 1], None, ALU.mult)
                            else:
                                dve.wait_ge(conv_ok, done + 2 * (j - 1) + i + 1)
                                op = nc.vector.scalar_tensor_tensor(acc, src, taps[:, m, tap:tap + 1], acc, ALU.mult, ALU.add)
                            op.then_inc(conv_ok, 1)
                elif k < 18:
                    m = (k - 11) // 2
                    if m == 0 and not (isinstance(g, int) and g < 2):
                        tile_read(dve, back_tile(g - 2, B_FFN + 1))
                    move(gate[:, gp, m, :], front_tile(g, F_GATE + m))
                elif k == 18:
                    move(dt_in, front_tile(g, F_DTIN))
                elif k < 23:
                    m = k - 19
                    if m == 0:
                        dve.wait_ge(u_ok, MT * (g + 1))
                    ps, read = read_tile(front_tile(g, F_DT + m))
                    nc.vector.tensor_scalar(sp_lin[:, m, :], ps, dt_bias[:, m:m + 1], None, ALU.add).then_inc(read, 1)
                elif k == 23:
                    wait(dve, c_stored, 16 * g)
                    move(bcT[0:2 * NSTATE, :], front_tile(g, F_BC), view=lambda ps: ps[0:2 * NSTATE, :])
                elif k < 26:
                    h = k - 24
                    move(b_col[:, gp, 2 * h:2 * h + 2, :].rearrange("p b n -> p (b n)"), front_tile(g, F_BT + h),
                         view=lambda ps: ps[:, 0:2 * NSTATE])
                else:
                    h = slice(HT * (k - 26), HT * (k - 25))
                    dve.wait_ge(sp_ln, g + 1)
                    nc.vector.scalar_tensor_tensor(sp_lin[:, :, h], sp_lin[:, :, h], 0.0, sp_log[:, :, h],
                                                   ALU.max, ALU.add).then_inc(dt_new, 1)

            def back_piece(g, k):
                gp = g % 2
                kT, omax, ev_upd, ev_out = dead_gate(gp, 0), dead_u(gp, 0), dead_u(gp, 1), dead_gate(gp, 1)
                prev = oprev[:, :, :].rearrange("p s t -> p (s t)")
                halves = [slice(c * TOK, (c + 1) * TOK) for c in range(CT)]
                if k < 2:
                    h = slice(HT * k, HT * k + HT)
                    if k == 0:
                        dve.wait_ge(sum_ok, SUMS * (g + 1))
                        if not (isinstance(g, int) and g == GROUPS - 1):
                            dve.wait_ge(dt_ok, g + 2)
                    for m in range(MT):
                        nc.vector.scalar_tensor_tensor(z[:, m, h], u[:, gp, m, h], skip[:, m:m + 1], psY[:, m, h],
                                                       ALU.mult, ALU.add).then_inc(skip_ok, 1)
                elif k in (2, 5):
                    h = (k - 2) // 3
                    hs = slice(HB * h, HB * h + HB)
                    if h == 0:
                        dve.wait_ge(ld_x2, 16 * (g + 1))
                    ps, read = read_tile(back_tile(g, B_OUT + h))
                    nc.vector.tensor_tensor(x2[:, hs, :], x2[:, hs, :], ps.rearrange("p (b c) -> p b c", b=HB), ALU.add).then_inc(read, 1)
                elif k in (3, 6):
                    h = (k - 3) // 3
                    tile_read(dve, back_tile(g, B_OUT + h))
                    variances(1, 4 * g + h, h, x2)
                elif k in (4, 7):
                    normalise(1, 4 * g + (k - 4) // 3, (k - 4) // 3, x2)
                elif k < 10:
                    move(kT[:, (k - 8) * TOK:(k - 7) * TOK], back_tile(g, B_KT + k - 8))
                elif k == 10:
                    tile_read(dve, back_tile(g, B_KT + CT - 1))
                    nc.vector.tensor_tensor_scan(omax, decay_row[:, :, :, :].rearrange("p c b t -> p (c b t)"), kT, 0.0,
                                                 ALU.add, ALU.max).then_inc(omax_ok, 1)
                elif k == 11:
                    dve.wait_ge(omax_ok, g + 1)
                    nc.vector.tensor_tensor(ex_upd[:, 1], kT, omax, ALU.subtract).then_inc(upd_arg, 1)
                    dve.wait_ge(oprev_ok, g + 1)
                    for c, h in enumerate(halves):
                        nc.vector.scalar_tensor_tensor(ex_upd[:, 0, h], prev[:, h], decay_w[:, c:c + 1], omax[:, h],
                                                       ALU.add, ALU.subtract).then_inc(upd_arg, 1)
                elif k == 12:
                    for c, h in enumerate(halves):
                        nc.vector.scalar_tensor_tensor(onew[:, h], kT[:, h], bonus_u[:, c:c + 1], prev[:, h],
                                                       ALU.add, ALU.max).then_inc(out_arg, 1)
                    for c, h in enumerate(halves):
                        dve.wait_ge(out_arg, 5 * g + c + 1)
                        nc.vector.scalar_tensor_tensor(ex_out[:, 1, h], kT[:, h], bonus_u[:, c:c + 1], onew[:, h],
                                                       ALU.add, ALU.subtract).then_inc(out_arg, 1)
                    nc.vector.tensor_tensor(ex_out[:, 0], prev, onew, ALU.subtract).then_inc(out_arg, 1)
                elif k == 13:
                    dve.wait_ge(upd_exp, g + 1)
                    nc.vector.memset(pq[:, :, 0:1], 0.0).then_inc(pq_zero, 1)
                    nc.vector.tensor_tensor_scan(qbuf[:, 1:], ex_upd[:, 0], ex_upd[:, 1], 0.0, ALU.mult, ALU.add).then_inc(q_ok, 1)
                elif k == 14:
                    dve.wait_ge(ev_upd_ok, g + 1)
                    nc.vector.tensor_tensor_scan(pbuf[:, 1:], ex_upd[:, 0], ev_upd, 0.0, ALU.mult, ALU.add).then_inc(p_ok, 1)
                elif k == 15:
                    den, num = omax, kT
                    dve.wait_ge(out_exp, g + 1)
                    dve.wait_ge(q_ok, g + 1)
                    dve.wait_ge(pq_zero, g + 1)
                    nc.vector.tensor_tensor(den, ex_out[:, 0], qbuf[:, 0:CT * TOK], ALU.mult).then_inc(den_ok, 1)
                    dve.wait_ge(p_ok, g + 1)
                    nc.vector.tensor_tensor(num, ex_out[:, 0], pbuf[:, 0:CT * TOK], ALU.mult).then_inc(num_ok, 1)
                    dve.wait_ge(den_ok, 2 * g + 1)
                    nc.vector.tensor_tensor(den, den, ex_out[:, 1], ALU.add).then_inc(den_ok, 1)
                    dve.wait_ge(ev_out_ok, g + 1)
                    dve.wait_ge(num_ok, 2 * g + 1)
                    nc.vector.tensor_tensor(num, num, ev_out, ALU.add).then_inc(num_ok, 1)
                elif k == 16:
                    den, num, r = omax, kT, ex_upd[:, 0]
                    dve.wait_ge(rec_ok, 2 * (g + 1))
                    nc.vector.tensor_tensor(den, den, r, ALU.mult).then_inc(y_ok, 1)
                    dve.wait_ge(num_ok, 2 * (g + 1))
                    nc.vector.tensor_tensor(num, num, r, ALU.mult).then_inc(y_ok, 1)
                    dve.wait_ge(y_ok, 3 * g + 2)
                    nc.vector.scalar_tensor_tensor(onew, den, 2.0, num, ALU.subtract, ALU.mult).then_inc(y_ok, 1)
                elif k < 23:
                    h, step = divmod(k - 17, 3)
                    hs = slice(HB * h, HB * h + HB)
                    if step == 0:
                        ps, read = read_tile(back_tile(g, B_YT + h))
                        nc.vector.tensor_tensor(x2[:, hs, :], x2[:, hs, :], ps.rearrange("p (b c) -> p b c", b=HB),
                                                ALU.subtract).then_inc(read, 1)
                    elif step == 1:
                        tile_read(dve, back_tile(g, B_YT + h))
                        variances(1, 4 * g + 2 + h, h, x2)
                    else:
                        normalise(1, 4 * g + 2 + h, h, x2)
                elif k < 25:
                    h = k - 23
                    move(x3T[:, :, HT * h:HT * h + HT], back_tile(g, B_X3T + h), view=lambda ps: ps.rearrange("p (c t) -> p c t", c=CT))
                else:
                    hs = slice(HB * (k - 25), HB * (k - 25) + HB)
                    x3b = dead_gate(gp, 0).rearrange("p (b c) -> p b c", b=NB)
                    if k == 25:
                        dve.wait_ge(x3b_ok, g + 1)
                    ps, read = read_tile(back_tile(g, B_FFN + k - 25))
                    nc.vector.tensor_tensor(outb[:, hs, :], x3b[:, hs, :], ps.rearrange("p (b c) -> p b c", b=HB), ALU.add).then_inc(read, 1)

            def scan_step(g, n, m):
                slot = SLOTS * g + MT * n + m
                if m == 0:
                    lap, old = divmod(n - STATE_RING, NSTATE)
                    if old + 1 in PAIRED:
                        wait(dve, pair_ok, PAIRS * g + PAIRS * lap + pairs_to(old + 1) if not (isinstance(g, int) and g + lap < 0) else 0)
                    else:
                        wait(dve, sum_ok, SUMS * g + SUMS * lap + sums_to(old) if not (isinstance(g, int) and g + lap < 0) else 0)
                dve.wait_ge(decay_ok, slot + 1)
                dve.wait_ge(ring_ok, slot + 1)
                nc.vector.tensor_tensor_scan(state[:, n % STATE_RING, m, :], decay[:, n % 2, m].rearrange("p b t -> p (b t)"),
                                             psR[:, m % 2, :], 0.0, ALU.mult, ALU.add).then_inc(scan_ok, 1)

            nc.vector.memset(ones, 1.0).then_inc(dve_init, 1)
            nc.vector.memset(decay[:, :, :, :, 0:1].rearrange("p a m b o -> p (a m b) o"), 0.0).then_inc(dve_init, 1)
            nc.vector.memset(oprev[:, :, 0:1], NEG_INF).then_inc(dve_init, 1)
            nc.vector.memset(decay_row[:, :, :, :], 0.0).then_inc(dve_init, 1)
            dve.wait_ge(ld["vec"], VEC_LOADS * 16)
            dve.wait_ge(dve_init, 4)
            for c in range(CT):
                nc.vector.tensor_scalar(decay_row[:, c], decay_row[:, c], decay_w[:, c:c + 1], None, ALU.add).then_inc(dve_init, 1)
            dve.wait_ge(dve_init, 4 + CT)
            nc.vector.memset(decay_row[:, :, :, 0:1].rearrange("p c b o -> p (c b) o"), NEG_INF).then_inc(dve_init, 1)
            dve.wait_ge(dve_init, INIT_STEPS)
            for k in range(18):
                if k == 12:
                    dve.wait_ge(ld["w_ffn"], 16)
                    nc.vector.tensor_reduce(small[:, 0:1], w_ffn.rearrange("p o i -> p (o i)"), AX_X, ALU.add,
                                            apply_absolute_value=True).then_inc(tern_dve, 1)
                if k not in (6, 7, 8, 9) and not (k > 10 and k % 2):
                    front_piece(0, k)
            dve.wait_ge(tern_pe, 1)
            nc.vector.tensor_scalar(small[:, 1:2], psR[:, 0, 0:1], 1.0 / (HID * HID), None, ALU.mult).then_inc(tern_dve, 1)
            for k in range(18, 26):
                front_piece(0, k)
            dve.wait_ge(tern_dve, 2)
            nc.vector.tensor_scalar(small[:, 2:3], small[:, 1:2], TERNARY_EPS, None, ALU.add).then_inc(tern_dve, 1)
            dve.wait_ge(tern_dve, 3)
            nc.vector.reciprocal(small[:, 3:4], small[:, 2:3]).then_inc(tern_dve, 1)
            dve.wait_ge(tern_dve, 4)
            nc.vector.tensor_scalar(w_ffnT[:, :, :], w_ffn, small[:, 3:4], 1.0, ALU.mult, ALU.min).then_inc(tern_dve, 1)
            dve.wait_ge(tern_dve, 5)
            nc.vector.tensor_scalar(w_ffnT[:, :, :], w_ffnT[:, :, :], -1.0, ROUND_MAGIC, ALU.max, ALU.add).then_inc(tern_dve, 1)
            dve.wait_ge(tern_dve, 6)
            nc.vector.tensor_scalar(w_ffnT[:, :, :], w_ffnT[:, :, :], ROUND_MAGIC, small[:, 1:2], ALU.subtract, ALU.mult).then_inc(tern_dve, 1)
            dve.wait_ge(tern_dve, 7)
            nc.vector.tensor_tensor(w_ffnT[:, :, :], w_ffnT[:, :, :], w_ffn, ALU.subtract).then_inc(tern_dve, 1)
            dve.wait_ge(tern_dve, 8)
            nc.vector.tensor_tensor(w_ffnT[:, :, :], w_ffnT[:, :, :], w_ffn, ALU.add).then_inc(tern_dve, 1)
            for k in (26, 27):
                front_piece(0, k)
                h = slice(HT * (k - 26), HT * (k - 25))
                dve.wait_ge(dt_new, k - 25)
                nc.vector.tensor_tensor(dtu[:, :, h], sp_lin[:, :, h], u[:, 0, :, h], ALU.mult).then_inc(dtu_ok, 1)

            def iteration(g, back, front):
                for n in range(NSTATE):
                    for m in range(MT):
                        scan_step(g, n, m)
                        if back:
                            pieces(DVE_BACK, MT * n + m, back_piece, g - 1)
                        if front:
                            pieces(DVE_FRONT, MT * n + m, front_piece, g + 1)

            iteration(0, False, True)
            with dve.Fori(1, GROUPS - 1) as g:
                iteration(g, True, True)
            iteration(GROUPS - 1, True, False)
            for k in (0, 100, 1, 101, *range(2, 27)):
                if k < 100:
                    back_piece(GROUPS - 1, k)
                else:
                    h = slice(HT * (k - 100), HT * (k - 99))
                    dve.wait_ge(skip_ok, 2 * MT * (GROUPS - 1) + MT * (k - 99))
                    nc.vector.tensor_tensor(z[:, :, h], z[:, :, h], gate[:, (GROUPS - 1) % 2, :, h], ALU.mult).then_inc(z_ok, 1)

        @block.gpsimd
        def _(pool):
            def front_piece(g, h):
                hs = slice(HT * h, HT * h + HT)
                pool.wait_ge(dt_new, 2 * g + h + 1)
                nc.gpsimd.tensor_tensor(dtu[:, :, hs], sp_lin[:, :, hs], u[:, g % 2, :, hs], ALU.mult).then_inc(dtu_ok, 1)

            def back_piece(g, k):
                gp = g % 2
                if k < 2:
                    hs = slice(HT * k, HT * k + HT)
                    pool.wait_ge(skip_ok, 2 * MT * g + MT * (k + 1))
                    nc.gpsimd.tensor_tensor(z[:, :, hs], z[:, :, hs], gate[:, gp, :, hs], ALU.mult).then_inc(z_ok, 1)
                elif k == 2:
                    pool.wait_ge(upd_exp, g + 1)
                    pool.wait_ge(ld_ctx, 16 * (g + 1))
                    nc.gpsimd.tensor_tensor(dead_u(gp, 1), ex_upd[:, 1], vT[:, :], ALU.mult).then_inc(ev_upd_ok, 1)
                elif k == 3:
                    pool.wait_ge(out_exp, g + 1)
                    nc.gpsimd.tensor_tensor(dead_gate(gp, 1), ex_out[:, 1], vT[:, :], ALU.mult).then_inc(ev_out_ok, 1)
                else:
                    tile_read(pool, back_tile(g, B_YT + 1))
                    hold_wait(pool)
                    nc.gpsimd.tensor_tensor(dead_gate(gp, 0).rearrange("p (b c) -> p b c", b=NB), x2[:, :, :],
                                            ffn_bias[:, :].rearrange("p (o c) -> p o c", o=1).broadcast_to((P, NB, HID)),
                                            ALU.add).then_inc(x3b_ok, 1)

            def product_step(g, n):
                pool.wait_ge(ld_c[n % C_RING], 16 * (NSTATE // C_RING * g + n // C_RING + 1))
                s = state[:, n % STATE_RING]
                if n == NSTATE - 1:
                    for m in range(MT):
                        pool.wait_ge(scan_ok, SLOTS * g + MT * n + m + 1)
                        nc.gpsimd.tensor_tensor(s[:, m, :], s[:, m, :], c_rep[:, n % C_RING, :], ALU.mult).then_inc(prod_ok, 1)
                else:
                    pool.wait_ge(scan_ok, MT * (NSTATE * g + n + 1))
                    nc.gpsimd.tensor_tensor(s, s, c_rep[:, n % C_RING:n % C_RING + 1, :].broadcast_to((P, MT, TOK)),
                                            ALU.mult).then_inc(prod_ok, 1)
                if n in PAIRED:
                    pool.wait_ge(prod_ok, PRODS * g + n + 1)
                    nc.gpsimd.tensor_tensor(s, s, state[:, (n - 1) % STATE_RING], ALU.add).then_inc(pair_ok, 1)

            nc.gpsimd.memset(ident[:, :], 0.0).then_inc(pool_init, 1)
            pool.wait_ge(pool_init, 1)
            nc.gpsimd.affine_select(out=ident[:, :], in_=ident[:, :], compare_op=ALU.not_equal, fill=1.0, base=0,
                                    pattern=[[-1, P]], channel_multiplier=1).then_inc(pool_init, 1)
            def iteration(g, back, front):
                for n in range(NSTATE):
                    product_step(g, n)
                    if back:
                        pieces(POOL_BACK, n, back_piece, g - 1)
                    if front:
                        pieces(POOL_FRONT, n, front_piece, g + 1)

            iteration(0, False, True)
            with pool.Fori(1, GROUPS - 1) as g:
                iteration(g, True, True)
            iteration(GROUPS - 1, True, False)
            for k in (2, 3, 4):
                back_piece(GROUPS - 1, k)


_INS = ["x", "ctx_2048", "L0_attn_in_proj_w", "L0_attn_conv_w", "L0_attn_conv_b", "L0_attn_x_proj_w",
        "L0_attn_dt_proj_w", "L0_attn_dt_proj_b", "L0_attn_A_log", "L0_attn_D", "L0_attn_out_proj_w",
        "L0_xattn_w", "L0_xattn_u", "L0_ffn_weight", "L0_ffn_bias"]

_VECTORS = ["L0_attn_conv_b", "L0_attn_dt_proj_b", "L0_attn_D", "L0_xattn_w", "L0_xattn_u"]


def kernel(**inputs):
    import numpy as np
    from concourse import bacc
    from concourse.bass_utils import run_bass_kernel_spmd

    nc = bacc.Bacc("TRN2", target_bir_lowering=False, num_devices=1)
    arrays, args = {}, []
    for name in _INS:
        a = np.asarray(inputs[name])
        if name == "ctx_2048":
            a = a.transpose(2, 0, 1).reshape(a.shape[2], -1)
        elif name == "L0_ffn_weight":
            a = a.T
        elif name in _VECTORS:
            a = a.reshape(-1, P).T
        a = np.ascontiguousarray(a)
        arrays[f"in_{name}"] = a
        args.append(nc.dram_tensor(f"in_{name}", a.shape, mybir.dt.from_np(a.dtype), kind="ExternalInput").ap())
    shape = tuple(inputs["x"].shape)
    args.append(nc.dram_tensor("out_0", shape, F32, kind="ExternalOutput").ap())
    build_decoder(nc, *args)
    r = run_bass_kernel_spmd(nc, [arrays], core_ids=[0])
    return r.results[0]["out_0"]
```

```python
from contextlib import ExitStack

from concourse import mybir
from concourse.alu_op_type import AluOpType as ALU

F32 = mybir.dt.float32
I32 = mybir.dt.int32
ACT = mybir.ActivationFunctionType
AX_X = mybir.AxisListType.X

P = 128
LN_EPS = 1e-5
TERNARY_EPS = 1e-10
ROUND_MAGIC = 12582912.0
NEG_INF = -1e38
RSQRT_GUESS = float(0x5F3759DF)
NEWTON = 3
VEC_LOADS = 8
WARM_UP = 40
INIT_STEPS = 7
TERN_STEPS = 9


def build_decoder(nc, x, ctxT, in_proj_w, conv_w, conv_b, x_proj_w, dt_proj_w, dt_proj_b, A_log, D_skip,
                  out_proj_w, wkv_w, wkv_u, ffn_wT, ffn_b, out):
    BATCH, T, HID = x.shape
    INTER, NSTATE = A_log.shape
    RANK = dt_proj_w.shape[0]
    KCONV = conv_w.shape[2]
    assert T == P and RANK == P
    NB = 4
    GROUPS = BATCH // NB
    TOK = NB * T
    MT = INTER // P
    CT = HID // P
    SLOTS = NSTATE * MT
    STATE_RING, C_RING = 4, 4
    PAIRED = (9, 11)
    PAIRS, SUMS = len(PAIRED), NSTATE - len(PAIRED)
    PRODS = 2 * (NSTATE - 1) + MT

    def prods_to(n):
        return 2 * (n + 1) if n < NSTATE - 1 else PRODS

    def pairs_to(n):
        return sum(k <= n for k in PAIRED)

    def sums_to(n):
        return n + 1 - sum(k <= n + 1 for k in PAIRED)

    def sums_due(n):
        return [k for k in (n - 3, n - 2) if 0 <= k < NSTATE and k + 1 not in PAIRED and (k == n - 3) == (k in PAIRED)]

    HB = NB // 2
    HT = HB * T
    LN_STEPS = 2 * NB + 3 + 3 * NEWTON

    FRONT_TILES, BACK_TILES = 22, 10
    F_XNT, F_HID, F_GATE, F_DTIN, F_DT, F_BC, F_BT, F_DTUT = 0, 2, 6, 10, 11, 15, 16, 18
    B_OUT, B_KT, B_YT, B_X3T, B_FFN = 0, 2, 4, 6, 8
    RING, FRONT_BANK, BACK_BANK = MT, MT + 2, MT + 3
    FIRST_BANKS = (FRONT_BANK, 0, 1, 2, 3, BACK_BANK)
    LAST_BANKS = (BACK_BANK, FRONT_BANK, 0, 1, 2, 3)

    def first_turns(bank):
        return len(range(FIRST_BANKS.index(bank), FRONT_TILES, len(FIRST_BANKS)))

    def front_tile(g, k):
        if isinstance(g, int) and g == 0:
            return FIRST_BANKS[k % len(FIRST_BANKS)], k // len(FIRST_BANKS)
        return FRONT_BANK, FRONT_TILES * g + (first_turns(FRONT_BANK) - FRONT_TILES + k)

    def back_tile(g, k):
        if isinstance(g, int) and g == GROUPS - 1:
            bank, before = LAST_BANKS[k % len(LAST_BANKS)], k // len(LAST_BANKS)
            before += {BACK_BANK: BACK_TILES * g, FRONT_BANK: FRONT_TILES * (GROUPS - 1)}.get(bank, 0)
            return bank, first_turns(bank) + before
        return BACK_BANK, BACK_TILES * g + (first_turns(BACK_BANK) + k)

    with ExitStack() as ctx:
        def sb(name, shape):
            return ctx.enter_context(nc.sbuf_tensor(name, shape, F32))

        def sem(name):
            return ctx.enter_context(nc.semaphore(name))

        def wait(eng, s, count):
            if not (isinstance(count, int) and count <= 0):
                eng.wait_ge(s, count)

        ident = sb("ident", [P, P])
        w_in = sb("w_in", [P, CT, 2 * INTER])
        w_x = sb("w_x", [P, MT, RANK + 2 * NSTATE])
        w_dt = sb("w_dt", [P, INTER])
        w_out = sb("w_out", [P, MT, HID])
        w_ffnT = sb("w_ffnT", [P, CT, HID])
        ffn_bias = sb("ffn_bias", [P, HID])
        taps = sb("taps", [P, MT, KCONV])
        conv_bias = sb("conv_bias", [P, MT])
        dt_bias = sb("dt_bias", [P, MT])
        skip = sb("skip", [P, MT])
        A_neg = sb("A_neg", [P, MT, NSTATE])
        decay_w = sb("decay_w", [P, CT])
        bonus_u = sb("bonus_u", [P, CT])
        decay_row = sb("decay_row", [P, CT, NB, T])
        small = sb("small", [P, 4])

        xin = sb("xin", [P, NB, HID])
        stats = [sb("stats_f", [P, NB, 6]), sb("stats_b", [P, NB, 6])]
        meanvar = [sb("meanvar_f", [P, NB, 2]), sb("meanvar_b", [P, NB, 2])]
        rstd = [sb("rstd_f", [P, 3, NB]), sb("rstd_b", [P, 3, NB])]
        xn = [sb("xn_f", [P, NB, HID]), sb("xn_b", [P, NB, HID])]
        xnT = sb("xnT", [P, CT, TOK])
        room_hpq = sb("room_hpq", [P, 2 * (1 + CT * TOK)])
        conv = sb("conv", [P, MT, TOK])
        u = sb("u", [P, 2, MT, TOK])
        gate = sb("gate", [P, 2, MT, TOK])
        bcT = sb("bcT", [P, TOK])
        b_col = sb("b_col", [P, 2, NB, NSTATE])
        sp_log = sb("sp_log", [P, MT, TOK])
        dt = sb("dt", [P, MT, NB, T])
        dtuT = sb("dtuT", [P, NB, INTER])

        decay = sb("decay", [P, 2, MT, NB, T])
        inT = sb("inT", [P, 2, NB, INTER])
        state = sb("state", [P, STATE_RING, MT, TOK])
        c_rep = sb("c_rep", [P, C_RING, TOK])

        x2 = sb("x2", [P, NB, HID])
        onew = sb("onew", [P, CT * TOK])[:, :]
        vT = sb("vT", [P, CT * TOK])
        x3T = sb("x3T", [P, CT, TOK])
        oprev = sb("oprev", [P, CT * NB, T])

        hidden = room_hpq[:, 0:MT * TOK].rearrange("p (m b t) -> p m b t", m=MT, b=NB)
        pq = room_hpq[:, :].rearrange("p (a s) -> p a s", a=2)
        pbuf, qbuf = pq[:, 0, :], pq[:, 1, :]
        sp_lin = conv
        dtu = sp_log
        dt_in = xn[0][:, 0:2, :].rearrange("p b c -> p (b c)")
        z = conv
        ex_upd = sp_log[:, :, :].rearrange("p (h c) t -> p h (c t)", h=2)
        ex_out = conv[:, :, :].rearrange("p (h c) t -> p h (c t)", h=2)
        outb = vT[:, :].rearrange("p (b c) -> p b c", b=NB)
        w_ffn = x2[:, 0:CT, :]
        ones = vT[:, 0:P]

        def dead_gate(gp, half):
            return gate[:, gp, CT * half:CT * half + CT, :].rearrange("p c t -> p (c t)")

        def dead_u(gp, half):
            return u[:, gp, CT * half:CT * half + CT, :].rearrange("p c t -> p (c t)")

        psum = ctx.enter_context(nc.psum_tensor("psum", [P, MT + 4, TOK], F32))
        psY, psR = psum[:, 0:MT], psum[:, RING:RING + 2]

        c_dram = nc.dram_tensor("c_rows", (GROUPS, NSTATE, TOK), F32, kind="Internal").ap()

        ld = {k: sem("ld_" + k) for k in ("vec", "w_in", "w_x", "w_dt", "w_out", "w_ffn")}
        ld_x, ld_x2, ld_ctx, ld_c = [sem("ld_x0"), sem("ld_x1")], sem("ld_x2"), sem("ld_ctx"), [sem(f"ld_c{i}") for i in range(C_RING)]
        c_stored, room_v_free = sem("c_stored"), sem("room_v_free")
        pool_init, dve_init, a_init = sem("pool_init"), sem("dve_init"), sem("a_init")
        tern_dve, tern_pe = sem("tern_dve"), sem("tern_pe")
        bank_done = {b: sem(f"bank{b}_done") for b in FIRST_BANKS}
        bank_read = {b: sem(f"bank{b}_read") for b in FIRST_BANKS}
        ln_dve = [sem("ln_dve_f"), sem("ln_dve_b")]
        xn_ok = [sem("xn_f_ok"), sem("xn_b_ok")]
        conv_ok, u_ok, sp_exp, sp_ln, dt_ok, dtu_ok, dt_new = (sem("conv_ok"), sem("u_ok"), sem("sp_exp"), sem("sp_ln"),
                                                       sem("dt_ok"), sem("dtu_ok"), sem("dt_new"))
        decay_ok, inT_ok, ring_ok, scan_ok, prod_ok, sum_ok = (sem("decay_ok"), sem("inT_ok"), sem("ring_ok"),
                                                              sem("scan_ok"), sem("prod_ok"), sem("sum_ok"))
        pair_ok = sem("pair_ok")
        skip_ok, z_ok, omax_ok, oprev_ok = sem("skip_ok"), sem("z_ok"), sem("omax_ok"), sem("oprev_ok")
        upd_arg, upd_exp, out_arg, out_exp = sem("upd_arg"), sem("upd_exp"), sem("out_arg"), sem("out_exp")
        ev_upd_ok, ev_out_ok, p_ok, q_ok = sem("ev_upd_ok"), sem("ev_out_ok"), sem("p_ok"), sem("q_ok")
        den_ok, rec_ok, num_ok, y_ok = sem("den_ok"), sem("rec_ok"), sem("num_ok"), sem("y_ok")
        x3b_ok, pq_zero = sem("x3b_ok"), sem("pq_zero")

        x_g = x.rearrange("(g b) t c -> g t b c", b=NB)
        ctx_g = ctxT.rearrange("(c p) (g t) -> g p c t", p=P, g=GROUPS)
        out_g = out.rearrange("(g b) t c -> g t b c", b=NB)

        def tile_done(eng, tile):
            bank, turn = tile
            eng.wait_ge(bank_done[bank], turn + 1)

        def tile_read(eng, tile):
            bank, turn = tile
            eng.wait_ge(bank_read[bank], turn + 1)

        PE_BACK = {8: [0], 9: [1], 15: [2], 16: [3], 30: [4], 31: [5], 38: [6], 39: [7, 8], 42: [9]}
        PE_FRONT = {35: [0], 39: [1], 41: [2], 42: [3], 43: [4, 5], 44: [6], 46: [7, 8], 49: [9, 10], 50: [11], 52: [12], 53: [13], 54: [14], 56: [15], 57: [16], 58: [17], 61: [18, 19], 62: [20], 63: [21]}
        ACT_BACK = {22: [0], 23: [1], 28: [2], 31: [3]}
        ACT_FRONT = {52: [0], 62: [1], 63: [2, 3, 4, 5]}
        DVE_BACK = {3: [0], 6: [1], 7: [2], 8: [3], 9: [4], 10: [5], 11: [6, 7], 12: [8], 16: [9, 10, 11], 18: [12, 13], 21: [14, 15, 16], 23: [17], 25: [18, 19], 26: [20], 28: [21, 22, 23], 30: [24, 25], 31: [26, 27], 33: [28, 29], 37: [30, 31], 38: [32], 40: [33], 43: [34]}
        DVE_FRONT = {22: [0], 26: [1, 2], 32: [3], 33: [4], 36: [5], 39: [6], 41: [7], 42: [8], 43: [9, 10], 44: [11, 12, 13, 14], 45: [15, 16, 17, 18], 48: [19, 20, 21, 22], 49: [23], 51: [24], 52: [25, 26], 55: [27], 56: [28], 57: [29], 58: [30], 59: [31], 60: [32]}
        POOL_BACK = {0: [0, 1], 4: [2], 5: [3, 4, 5], 8: [6]}
        POOL_FRONT = {13: [0, 1]}
        SP_BACK = {12: [1]}
        SP_FRONT = {3: [0], 14: [1]}

        def pieces(table, at, piece, g):
            for k in table.get(at, []):
                piece(g, k)

        def hold_wait(eng):
            eng.nop(nofuse=True)

        block = ctx.enter_context(nc.Block())

        @block.sync
        def _(sp):
            def front_piece(g, k):
                if k == 0:
                    wait(sp, xn_ok[0], NB * g)
                    for h in range(2):
                        sp.dma_start(xin[:, HB * h:HB * h + HB, :], x_g[g][:, HB * h:HB * h + HB]).then_inc(ld_x[h], 16)
                else:
                    tile_read(sp, front_tile(g, F_BC))
                    sp.dma_start(c_dram[g], bcT[NSTATE:2 * NSTATE, :]).then_inc(c_stored, 16)

            def back_piece(g, k):
                if k == 0:
                    sp.wait_ge(tern_dve, TERN_STEPS)
                    if not (isinstance(g, int) and g == 0):
                        tile_read(sp, back_tile(g - 1, B_FFN + 1))
                    sp.dma_start(x2[:, :, :], x_g[g]).then_inc(ld_x2, 16)
                    sp.wait_ge(room_v_free, 2 * 16 * g + 1)
                    sp.dma_start(vT[:, :].rearrange("p (c t) -> p c t", c=CT), ctx_g[g]).then_inc(ld_ctx, 16)
                else:
                    for h in range(2):
                        tile_read(sp, back_tile(g, B_FFN + h))
                        sp.dma_start(out_g[g][:, 2 * h:2 * h + 2], outb[:, 2 * h:2 * h + 2]).then_inc(room_v_free, 16)

            def broadcast_c(g, n):
                lap, old = divmod(n - C_RING, NSTATE)
                wait(sp, prod_ok, PRODS * g + PRODS * lap + prods_to(old))
                if n == 0:
                    sp.wait_ge(c_stored, 16 * (g + 1))
                sp.dma_start(c_rep[:, n % C_RING, :], c_dram[g, n:n + 1, :].broadcast_to((P, TOK))).then_inc(ld_c[n % C_RING], 16)

            front_piece(0, 0)
            sp.dma_start(w_in[:, :, :], in_proj_w.rearrange("(k p) n -> p k n", p=P)).then_inc(ld["w_in"], 16)
            sp.dma_start(taps[:, :, :], conv_w.rearrange("(m p) a k -> p m (a k)", p=P)).then_inc(ld["vec"], 16)
            for dst, src in ((conv_bias, conv_b), (dt_bias, dt_proj_b), (skip, D_skip), (decay_w, wkv_w), (bonus_u, wkv_u)):
                sp.dma_start(dst[:, :], src).then_inc(ld["vec"], 16)
            sp.dma_start(A_neg[:, :, :], A_log.rearrange("(m p) n -> p m n", p=P)).then_inc(ld["vec"], 16)
            sp.dma_start(ffn_bias[:, :], ffn_b.rearrange("(a n) -> a n", a=1).broadcast_to((P, HID))).then_inc(ld["vec"], 16)
            sp.dma_start(w_x[:, :, :], x_proj_w.rearrange("(m p) n -> p m n", p=P)).then_inc(ld["w_x"], 16)
            sp.dma_start(w_dt[:, :], dt_proj_w).then_inc(ld["w_dt"], 16)
            sp.dma_start(w_ffn, ffn_wT.rearrange("(c p) o -> p c o", p=P)).then_inc(ld["w_ffn"], 16)
            sp.dma_start(w_out[:, :, :], out_proj_w.rearrange("(m p) n -> p m n", p=P)).then_inc(ld["w_out"], 16)
            front_piece(0, 1)

            def iteration(g, back, front):
                for n in range(NSTATE):
                    broadcast_c(g, n)
                    if back and n == 0:
                        back_piece(g - 1, 0)
                    if back:
                        pieces(SP_BACK, n, back_piece, g - 1)
                    if front:
                        pieces(SP_FRONT, n, front_piece, g + 1)

            iteration(0, False, True)
            with sp.Fori(1, GROUPS - 1) as g:
                iteration(g, True, True)
            iteration(GROUPS - 1, True, False)
            back_piece(GROUPS - 1, 0)
            back_piece(GROUPS - 1, 1)
            sp.wait_ge(room_v_free, 2 * 16 * GROUPS + 1)

        @block.tensor
        def _(pe):
            def open_tile(tile):
                bank, turn = tile
                wait(pe, bank_read[bank], turn)
                return psum[:, bank, :]

            def input_read(tile):
                if isinstance(tile[1], int):
                    tile_read(pe, tile)

            def transpose4(ps, src):
                for i in range(4):
                    last = nc.tensor.transpose(ps[:, i * P:(i + 1) * P], src(i), ident[:, :])
                return last

            def project(ps, lhs, rhs, ksteps):
                for k in range(ksteps):
                    last = nc.tensor.matmul(ps, lhs(k), rhs(k), start=(k == 0), stop=(k == ksteps - 1))
                return last

            def front_piece(g, k):
                first = isinstance(g, int) and g == 0
                gp = g % 2
                ps = open_tile(front_tile(g, k))
                if k < F_HID:
                    pe.wait_ge(xn_ok[0], NB * g + HB * (k + 1))
                    last = transpose4(ps, lambda i: xn[0][:, HB * k + i % HB, (i // HB) * P:(i // HB + 1) * P])
                elif k < F_DTIN:
                    if k == F_HID:
                        input_read(front_tile(g, F_XNT + 1))
                        if first:
                            pe.wait_ge(ld["w_in"], 16)
                    j = k - F_HID
                    last = project(ps, lambda c: w_in[:, c, j * P:(j + 1) * P], lambda c: xnT[:, c, :], CT)
                elif k == F_DTIN:
                    if first:
                        pe.wait_ge(ld["w_x"], 16)
                    for m in range(MT):
                        if first or m == 0:
                            pe.wait_ge(u_ok, MT * g + (m + 1 if first else MT))
                        last = nc.tensor.matmul(ps, w_x[:, m, 0:RANK], u[:, gp, m, :], start=(m == 0), stop=(m == MT - 1))
                elif k < F_BC:
                    input_read(front_tile(g, F_DTIN))
                    if first:
                        pe.wait_ge(ld["w_dt"], 16)
                    m = k - F_DT
                    last = project(ps, lambda _: w_dt[:, m * P:(m + 1) * P], lambda _: dt_in, 1)
                elif k == F_BC:
                    hold_wait(pe)
                    last = project(ps[0:2 * NSTATE, :], lambda m: w_x[:, m, RANK:RANK + 2 * NSTATE],
                                   lambda m: u[:, gp, m, :], MT)
                elif k < F_DTUT:
                    input_read(front_tile(g, F_BC))
                    hold_wait(pe)
                    for i in range(2):
                        b = 2 * (k - F_BT) + i
                        last = nc.tensor.transpose(ps[:, i * NSTATE:(i + 1) * NSTATE], bcT[0:NSTATE, b * T:(b + 1) * T],
                                                   ident[0:NSTATE, 0:NSTATE])
                else:
                    b = k - F_DTUT
                    pe.wait_ge(dtu_ok, 2 * g + b // HB + 1)
                    last = transpose4(ps, lambda m: dtu[:, m, b * T:(b + 1) * T])
                last.then_inc(bank_done[front_tile(g, k)[0]], 1)

            def back_piece(g, k):
                ps = open_tile(back_tile(g, k))
                if k < B_KT:
                    pe.wait_ge(z_ok, 2 * g + k - B_OUT + 1)
                    pe.wait_ge(ld["w_out"], 16)
                    for i in range(2):
                        b = 2 * (k - B_OUT) + i
                        last = project(ps[:, i * HID:(i + 1) * HID], lambda m: z[:, m, b * T:(b + 1) * T],
                                       lambda m: w_out[:, m, :], MT)
                elif k < B_YT:
                    c = k - B_KT
                    pe.wait_ge(xn_ok[1], NB * (2 * g + 1))
                    last = transpose4(ps, lambda b: xn[1][:, b, c * P:(c + 1) * P])
                elif B_X3T <= k < B_FFN:
                    h = k - B_X3T
                    pe.wait_ge(xn_ok[1], NB * (2 * g + 1) + HB * (h + 1))
                    last = transpose4(ps, lambda i: xn[1][:, HB * h + i % HB, (i // HB) * P:(i // HB + 1) * P])
                elif k < B_X3T:
                    pe.wait_ge(y_ok, 3 * (g + 1))
                    h = k - B_YT
                    last = transpose4(ps, lambda i: onew[:, (i % 2) * TOK + (2 * h + i // 2) * T:
                                                         (i % 2) * TOK + (2 * h + i // 2 + 1) * T])
                else:
                    input_read(back_tile(g, B_X3T + k - B_FFN))
                    for i in range(2):
                        b = 2 * (k - B_FFN) + i
                        last = project(ps[:, i * HID:(i + 1) * HID], lambda c: x3T[:, c, b * T:(b + 1) * T],
                                       lambda c: w_ffnT[:, c, :], CT)
                last.then_inc(bank_done[back_tile(g, k)[0]], 1)

            def scan_input(g, n, m):
                if m == 0:
                    pe.wait_ge(inT_ok, NB * (NSTATE * g + n + 1))
                wait(pe, scan_ok, SLOTS * g + MT * n + m - 1)
                transpose4(psR[:, m % 2, :], lambda b: inT[:, n % 2, b, m * P:(m + 1) * P]).then_inc(ring_ok, 1)

            def sum_states(g, n, m):
                half = m // 2
                if m % 2 == 0 and n in PAIRED:
                    pe.wait_ge(pair_ok, 2 * PAIRS * g + 2 * pairs_to(n) + half - 1)
                elif n == NSTATE - 1:
                    pe.wait_ge(prod_ok, PRODS * g + 2 * n + m + 1)
                elif m % 2 == 0:
                    pe.wait_ge(prod_ok, PRODS * g + 2 * n + half + 1)
                if n == 0:
                    if isinstance(g, int) and g == 0:
                        pe.wait_ge(bank_read[m], first_turns(m))
                    else:
                        pe.wait_ge(skip_ok, 2 * MT * g - MT + m + 1)
                last = nc.tensor.matmul(psY[:, m, :], ident[:, :], state[:, n % STATE_RING, m, :],
                                        start=(n == 0), stop=(n == NSTATE - 1))
                if m % 2:
                    last.then_inc(sum_ok, 1)

            pe.wait_ge(pool_init, 2)
            for _ in range(WARM_UP):
                nc.tensor.transpose(psR[:, 1, 0:P], ident[:, :], ident[:, :])
            for k in range(F_DTIN):
                front_piece(0, k)
            pe.wait_ge(tern_dve, 1)
            pe.wait_ge(dve_init, 1)
            nc.tensor.matmul(psR[:, 0, 0:P], ones, small[:, 0:1].broadcast_to((P, P)), start=True, stop=True).then_inc(tern_pe, 1)
            for k in range(F_DTIN, FRONT_TILES):
                front_piece(0, k)
            pe.wait_ge(tern_dve, 2)
            pe.nop(nofuse=True).then_inc(room_v_free, 1)

            def iteration(g, back, front):
                for n in range(NSTATE):
                    for m in range(MT):
                        scan_input(g, n, m)
                        for k in sums_due(n):
                            sum_states(g, k, m)
                        if back:
                            pieces(PE_BACK, MT * n + m, back_piece, g - 1)
                        if front:
                            pieces(PE_FRONT, MT * n + m, front_piece, g + 1)
                for n in sums_due(NSTATE) + sums_due(NSTATE + 1) + sums_due(NSTATE + 2):
                    for m in range(MT):
                        sum_states(g, n, m)

            iteration(0, False, True)
            with pe.Fori(1, GROUPS - 1) as g:
                iteration(g, True, True)
            iteration(GROUPS - 1, True, False)
            for k in range(BACK_TILES):
                back_piece(GROUPS - 1, k)

        @block.scalar
        def _(act):
            def evacuate(out_ap, tile, view=lambda ps: ps):
                bank, _ = tile
                tile_done(act, tile)
                nc.scalar.activation(out_ap, view(psum[:, bank, :]), ACT.Copy).then_inc(bank_read[bank], 1)

            def front_piece(g, k):
                gp = g % 2
                if k == 0:
                    if isinstance(g, int) and g == 0:
                        for m in range(MT):
                            silu_tile(m)
                    for m in range(MT):
                        act.wait_ge(conv_ok, MT * KCONV * g + 2 * KCONV * (m // 2) + 2 * (KCONV - 1) + m % 2 + 1)
                        nc.scalar.activation(u[:, gp, m, :], conv[:, m, :], ACT.Silu,
                                             bias=conv_bias[:, m:m + 1]).then_inc(u_ok, 1)
                    if not (isinstance(g, int) and g == 0):
                        tile_read(act, front_tile(g, F_GATE + MT - 1))
                        nc.scalar.activation(gate[:, gp], gate[:, gp], ACT.Silu)
                elif k == 1:
                    tile_read(act, front_tile(g, F_DT + MT - 1))
                    nc.scalar.activation(sp_log[:, :, :], sp_lin[:, :, :], ACT.Abs).then_inc(sp_exp, 1)
                    act.wait_ge(sp_exp, 2 * g + 1)
                    nc.scalar.activation(sp_log[:, :, :], sp_log[:, :, :], ACT.Exp, scale=-1.0).then_inc(sp_exp, 1)
                    act.wait_ge(sp_exp, 2 * g + 2)
                    nc.scalar.activation(sp_log[:, :, :], sp_log[:, :, :], ACT.Ln, bias=1.0).then_inc(sp_ln, 1)
                else:
                    b = k - 2
                    evacuate(dtuT[:, b, :], front_tile(g, F_DTUT + b))

            def silu_tile(m):
                bank, _ = front_tile(0, F_GATE + m)
                tile_done(act, front_tile(0, F_GATE + m))
                nc.scalar.activation(gate[:, 0, m, :], psum[:, bank, :], ACT.Silu).then_inc(bank_read[bank], 1)

            def copy_dt(g):
                act.wait_ge(dt_new, 2 * (g + 1))
                nc.scalar.activation(dt[:, :, :, :].rearrange("p m b t -> p m (b t)"), sp_lin[:, :, :],
                                     ACT.Copy).then_inc(dt_ok, 1)

            def back_piece(g, k):
                gp = g % 2
                if k == 0:
                    act.wait_ge(omax_ok, g + 1)
                    nc.scalar.activation(oprev[:, :, 1:T], dead_u(gp, 0).rearrange("p (s t) -> p s t", t=T)[:, :, 0:T - 1],
                                         ACT.Copy).then_inc(oprev_ok, 1)
                elif k == 1:
                    act.wait_ge(upd_arg, 3 * (g + 1))
                    nc.scalar.activation(ex_upd, ex_upd, ACT.Exp).then_inc(upd_exp, 1)
                elif k == 2:
                    act.wait_ge(out_arg, 5 * (g + 1))
                    nc.scalar.activation(ex_out, ex_out, ACT.Exp).then_inc(out_exp, 1)
                else:
                    act.wait_ge(den_ok, 2 * (g + 1))
                    act.wait_ge(p_ok, g + 1)
                    act.wait_ge(q_ok, g + 1)
                    hold_wait(act)
                    nc.scalar.activation(ex_upd[:, 0], dead_u(gp, 0), ACT.Ln).then_inc(rec_ok, 1)
                    act.wait_ge(rec_ok, 2 * g + 1)
                    nc.scalar.activation(ex_upd[:, 0], ex_upd[:, 0], ACT.Exp, scale=-1.0).then_inc(rec_ok, 1)

            def decay_step(g, n, m):
                src = dt if n else sp_lin[:, :, :].rearrange("p m (b t) -> p m b t", b=NB)
                if n == 0 and m == 0:
                    act.wait_ge(dt_new, 2 * (g + 1))
                if n == 1 and m == 0:
                    act.wait_ge(dt_ok, g + 1)
                if m == 0:
                    wait(act, scan_ok, MT * (NSTATE * g + n - 1))
                nc.scalar.activation(decay[:, n % 2, m, :, 1:T], src[:, m, :, 1:T], ACT.Exp,
                                     scale=A_neg[:, m, n:n + 1]).then_inc(decay_ok, 1)

            def input_step(g, n, b):
                if b == 0:
                    if n == 0:
                        tile_read(act, front_tile(g, F_DTUT + NB - 1))
                    wait(act, ring_ok, MT * (NSTATE * g + n - 1))
                nc.scalar.activation(inT[:, n % 2, b, :], dtuT[:, b, :], ACT.Copy,
                                     scale=b_col[:, g % 2, b, n:n + 1]).then_inc(inT_ok, 1)

            act.wait_ge(ld["vec"], VEC_LOADS * 16)
            nc.scalar.activation(A_neg[:, :, :], A_neg[:, :, :], ACT.Exp).then_inc(a_init, 1)
            act.wait_ge(a_init, 1)
            nc.scalar.activation(A_neg[:, :, :], A_neg[:, :, :], ACT.Copy, scale=-1.0).then_inc(a_init, 1)
            act.wait_ge(a_init, 2)
            for m in range(MT):
                evacuate(hidden[:, m], front_tile(0, F_HID + m), view=lambda ps: ps.rearrange("p (b t) -> p b t", b=NB))
            for k in range(6):
                front_piece(0, k)
            act.wait_ge(dve_init, INIT_STEPS)

            def iteration(g, back, front):
                for n in range(NSTATE):
                    for m in range(MT):
                        if n == 0 and m == 0:
                            for b in range(NB):
                                input_step(g, 0, b)
                        elif n > 0:
                            input_step(g, n, m)
                        decay_step(g, n, m)
                        if n == 0 and m == MT - 1:
                            copy_dt(g)
                        if back:
                            pieces(ACT_BACK, MT * n + m, back_piece, g - 1)
                        if front:
                            pieces(ACT_FRONT, MT * n + m, front_piece, g + 1)

            iteration(0, False, True)
            with act.Fori(1, GROUPS - 1) as g:
                iteration(g, True, True)
            iteration(GROUPS - 1, True, False)
            for k in range(4):
                back_piece(GROUPS - 1, k)

        @block.vector
        def _(dve):
            def read_tile(tile):
                bank, _ = tile
                tile_done(dve, tile)
                return psum[:, bank, :], bank_read[bank]

            def move(out_ap, tile, view=lambda ps: ps):
                ps, read = read_tile(tile)
                nc.vector.tensor_copy(out_ap, view(ps)).then_inc(read, 1)

            def variances(part, nth, h, src):
                st, mv, done = stats[part], meanvar[part], LN_STEPS * nth + 2 * HB * h
                for b in range(HB * h, HB * h + HB):
                    nc.vector.bn_stats(st[:, b, :], src[:, b, :]).then_inc(ln_dve[part], 1)
                dve.wait_ge(ln_dve[part], done + HB)
                hold_wait(dve)
                for b in range(HB * h, HB * h + HB):
                    nc.vector.bn_aggr(mv[:, b, :], st[:, b, :]).then_inc(ln_dve[part], 1)

            def inverse_deviations(part, nth, guess):
                rs, mv, done = rstd[part], meanvar[part], LN_STEPS * nth + 2 * NB
                v, t, r = rs[:, 0, :], rs[:, 1, :], rs[:, 2, :]
                if guess:
                    dve.wait_ge(ln_dve[part], done)
                    nc.vector.tensor_scalar(v, mv[:, :, 1], LN_EPS, None, ALU.add).then_inc(ln_dve[part], 1)
                    dve.wait_ge(ln_dve[part], done + 1)
                    nc.vector.tensor_scalar(t.bitcast(I32), v.bitcast(I32), 1, None, ALU.logical_shift_right).then_inc(ln_dve[part], 1)
                    dve.wait_ge(ln_dve[part], done + 2)
                    nc.vector.tensor_scalar(r.bitcast(I32), t.bitcast(I32), -1.0, RSQRT_GUESS, ALU.mult, ALU.add).then_inc(ln_dve[part], 1)
                for i in range(1) if guess else range(1, NEWTON):
                    dve.wait_ge(ln_dve[part], done + 3 * i + 3)
                    nc.vector.tensor_tensor(t, r, r, ALU.mult).then_inc(ln_dve[part], 1)
                    dve.wait_ge(ln_dve[part], done + 3 * i + 4)
                    nc.vector.scalar_tensor_tensor(t, t, -0.5, v, ALU.mult, ALU.mult).then_inc(ln_dve[part], 1)
                    dve.wait_ge(ln_dve[part], done + 3 * i + 5)
                    nc.vector.scalar_tensor_tensor(r, t, 1.5, r, ALU.add, ALU.mult).then_inc(ln_dve[part], 1)

            def normalise(part, nth, src):
                rs, mv = rstd[part], meanvar[part]
                dve.wait_ge(ln_dve[part], LN_STEPS * (nth + 1))
                for b in range(NB):
                    nc.vector.tensor_scalar(xn[part][:, b, :], src[:, b, :], mv[:, b, 0:1], rs[:, 2, b:b + 1],
                                            ALU.subtract, ALU.mult).then_inc(xn_ok[part], 1)

            def front_piece(g, k):
                gp = g % 2
                if k < 2:
                    dve.wait_ge(ld_x[k], 16 * (g + 1))
                    variances(0, g, k, xin)
                elif k < 4:
                    inverse_deviations(0, g, k == 2)
                elif k == 4:
                    normalise(0, g, xin)
                elif k < 7:
                    h = k - 5
                    move(xnT[:, :, HT * h:HT * h + HT], front_tile(g, F_XNT + h), view=lambda ps: ps.rearrange("p (c t) -> p c t", c=CT))
                elif k < 11:
                    m = k - 7
                    move(hidden[:, m], front_tile(g, F_HID + m), view=lambda ps: ps.rearrange("p (b t) -> p b t", b=NB))
                elif k < 23 and (k - 11) % 3 < 2:
                    half, first_tap = divmod((k - 11) // 3, 2)
                    j = 2 * first_tap + (k - 11) % 3
                    ms = (2 * half, 2 * half + 1)
                    done = MT * KCONV * g + 2 * KCONV * half
                    tap = KCONV - 1 - j
                    for i, m in enumerate(ms):
                        acc = conv[:, m, :].rearrange("p (b t) -> p b t", b=NB)[:, :, j:T]
                        src = hidden[:, m, :, 0:T - j]
                        if j == 0:
                            if i == 0:
                                tile_read(dve, front_tile(g, F_HID + ms[1]))
                            op = nc.vector.tensor_scalar(acc, src, taps[:, m, tap:tap + 1], None, ALU.mult)
                        else:
                            dve.wait_ge(conv_ok, done + 2 * (j - 1) + i + 1)
                            op = nc.vector.scalar_tensor_tensor(acc, src, taps[:, m, tap:tap + 1], acc, ALU.mult, ALU.add)
                        op.then_inc(conv_ok, 1)
                elif k < 23:
                    m = (k - 11) // 3
                    if m == 0 and not (isinstance(g, int) and g < 2):
                        tile_read(dve, back_tile(g - 2, B_FFN + 1))
                    move(gate[:, gp, m, :], front_tile(g, F_GATE + m))
                elif k == 23:
                    move(dt_in, front_tile(g, F_DTIN))
                elif k < 28:
                    m = k - 24
                    if m == 0:
                        dve.wait_ge(u_ok, MT * (g + 1))
                    ps, read = read_tile(front_tile(g, F_DT + m))
                    nc.vector.tensor_scalar(sp_lin[:, m, :], ps, dt_bias[:, m:m + 1], None, ALU.add).then_inc(read, 1)
                elif k == 28:
                    wait(dve, c_stored, 16 * g)
                    move(bcT[0:2 * NSTATE, :], front_tile(g, F_BC), view=lambda ps: ps[0:2 * NSTATE, :])
                elif k < 31:
                    h = k - 29
                    move(b_col[:, gp, 2 * h:2 * h + 2, :].rearrange("p b n -> p (b n)"), front_tile(g, F_BT + h),
                         view=lambda ps: ps[:, 0:2 * NSTATE])
                else:
                    h = slice(HT * (k - 31), HT * (k - 30))
                    dve.wait_ge(sp_ln, g + 1)
                    nc.vector.scalar_tensor_tensor(sp_lin[:, :, h], sp_lin[:, :, h], 0.0, sp_log[:, :, h],
                                                   ALU.max, ALU.add).then_inc(dt_new, 1)

            def residual_step(g, step, tile, nth, op):
                h = step // 2
                if step < 4 and step % 2 == 0:
                    hs = slice(HB * h, HB * h + HB)
                    if tile == B_OUT and h == 0:
                        dve.wait_ge(ld_x2, 16 * (g + 1))
                    ps, read = read_tile(back_tile(g, tile + h))
                    nc.vector.tensor_tensor(x2[:, hs, :], x2[:, hs, :], ps.rearrange("p (b c) -> p b c", b=HB), op).then_inc(read, 1)
                elif step < 4:
                    tile_read(dve, back_tile(g, tile + h))
                    variances(1, nth, h, x2)
                elif step < 6:
                    inverse_deviations(1, nth, step == 4)
                else:
                    normalise(1, nth, x2)

            def back_piece(g, k):
                gp = g % 2
                kT, omax, ev_upd = dead_gate(gp, 0), dead_u(gp, 0), dead_u(gp, 1)
                prev = oprev[:, :, :].rearrange("p s t -> p (s t)")
                halves = [slice(c * TOK, (c + 1) * TOK) for c in range(CT)]
                den, num, r = omax, kT, ex_upd[:, 0]
                if k < 2:
                    h = slice(HT * k, HT * k + HT)
                    if k == 0:
                        dve.wait_ge(sum_ok, 2 * SUMS * (g + 1))
                        if not (isinstance(g, int) and g == GROUPS - 1):
                            dve.wait_ge(dt_ok, g + 2)
                    for m in range(MT):
                        nc.vector.scalar_tensor_tensor(z[:, m, h], u[:, gp, m, h], skip[:, m:m + 1], psY[:, m, h],
                                                       ALU.mult, ALU.add).then_inc(skip_ok, 1)
                elif k < 9:
                    residual_step(g, k - 2, B_OUT, 2 * g, ALU.add)
                elif k < 11:
                    move(kT[:, (k - 9) * TOK:(k - 8) * TOK], back_tile(g, B_KT + k - 9))
                elif k == 11:
                    tile_read(dve, back_tile(g, B_KT + CT - 1))
                    nc.vector.tensor_tensor_scan(omax, decay_row[:, :, :, :].rearrange("p c b t -> p (c b t)"), kT, 0.0,
                                                 ALU.add, ALU.max).then_inc(omax_ok, 1)
                elif k == 12:
                    dve.wait_ge(omax_ok, g + 1)
                    nc.vector.tensor_tensor(ex_upd[:, 1], kT, omax, ALU.subtract).then_inc(upd_arg, 1)
                elif k == 13:
                    dve.wait_ge(oprev_ok, g + 1)
                    for c, h in enumerate(halves):
                        nc.vector.scalar_tensor_tensor(ex_upd[:, 0, h], prev[:, h], decay_w[:, c:c + 1], omax[:, h],
                                                       ALU.add, ALU.subtract).then_inc(upd_arg, 1)
                elif k == 14:
                    for c, h in enumerate(halves):
                        nc.vector.scalar_tensor_tensor(onew[:, h], kT[:, h], bonus_u[:, c:c + 1], prev[:, h],
                                                       ALU.add, ALU.max).then_inc(out_arg, 1)
                elif k == 15:
                    for c, h in enumerate(halves):
                        dve.wait_ge(out_arg, 5 * g + c + 1)
                        nc.vector.scalar_tensor_tensor(ex_out[:, 1, h], kT[:, h], bonus_u[:, c:c + 1], onew[:, h],
                                                       ALU.add, ALU.subtract).then_inc(out_arg, 1)
                elif k == 16:
                    nc.vector.tensor_tensor(ex_out[:, 0], prev, onew, ALU.subtract).then_inc(out_arg, 1)
                elif k == 17:
                    dve.wait_ge(upd_exp, g + 1)
                    nc.vector.memset(pq[:, :, 0:1], 0.0).then_inc(pq_zero, 1)
                    nc.vector.tensor_tensor_scan(qbuf[:, 1:], ex_upd[:, 0], ex_upd[:, 1], 0.0, ALU.mult, ALU.add).then_inc(q_ok, 1)
                elif k == 18:
                    dve.wait_ge(ev_upd_ok, g + 1)
                    nc.vector.tensor_tensor_scan(pbuf[:, 1:], ex_upd[:, 0], ev_upd, 0.0, ALU.mult, ALU.add).then_inc(p_ok, 1)
                elif k == 19:
                    dve.wait_ge(out_exp, g + 1)
                    dve.wait_ge(q_ok, g + 1)
                    dve.wait_ge(pq_zero, g + 1)
                    nc.vector.tensor_tensor(den, ex_out[:, 0], qbuf[:, 0:CT * TOK], ALU.mult).then_inc(den_ok, 1)
                elif k == 20:
                    dve.wait_ge(den_ok, 2 * g + 1)
                    nc.vector.tensor_tensor(den, den, ex_out[:, 1], ALU.add).then_inc(den_ok, 1)
                elif k == 21:
                    dve.wait_ge(rec_ok, 2 * (g + 1))
                    dve.wait_ge(num_ok, 2 * (g + 1))
                    nc.vector.tensor_tensor(num, num, r, ALU.mult).then_inc(y_ok, 1)
                elif k == 22:
                    nc.vector.tensor_tensor(den, den, r, ALU.mult).then_inc(y_ok, 1)
                elif k == 23:
                    dve.wait_ge(y_ok, 3 * g + 2)
                    nc.vector.scalar_tensor_tensor(onew, den, 2.0, num, ALU.subtract, ALU.mult).then_inc(y_ok, 1)
                elif k < 31:
                    residual_step(g, k - 24, B_YT, 2 * g + 1, ALU.subtract)
                elif k < 33:
                    h = k - 31
                    move(x3T[:, :, HT * h:HT * h + HT], back_tile(g, B_X3T + h), view=lambda ps: ps.rearrange("p (c t) -> p c t", c=CT))
                else:
                    hs = slice(HB * (k - 33), HB * (k - 33) + HB)
                    x3b = dead_gate(gp, 0).rearrange("p (b c) -> p b c", b=NB)
                    if k == 33:
                        dve.wait_ge(x3b_ok, g + 1)
                    ps, read = read_tile(back_tile(g, B_FFN + k - 33))
                    nc.vector.tensor_tensor(outb[:, hs, :], x3b[:, hs, :], ps.rearrange("p (b c) -> p b c", b=HB), ALU.add).then_inc(read, 1)

            def scan_step(g, n, m):
                slot = SLOTS * g + MT * n + m
                lap, old = divmod(n - STATE_RING, NSTATE)
                if m % 2 == 0 and not (isinstance(g, int) and g + lap < 0):
                    if old + 1 in PAIRED:
                        dve.wait_ge(pair_ok, 2 * PAIRS * g + 2 * PAIRS * lap + 2 * pairs_to(old + 1) + m // 2 - 1)
                    else:
                        dve.wait_ge(sum_ok, 2 * SUMS * g + 2 * SUMS * lap + 2 * sums_to(old) + m // 2 - 1)
                dve.wait_ge(decay_ok, slot + 1)
                dve.wait_ge(ring_ok, slot + 1)
                nc.vector.tensor_tensor_scan(state[:, n % STATE_RING, m, :], decay[:, n % 2, m].rearrange("p b t -> p (b t)"),
                                             psR[:, m % 2, :], 0.0, ALU.mult, ALU.add).then_inc(scan_ok, 1)

            nc.vector.memset(ones, 1.0).then_inc(dve_init, 1)
            nc.vector.memset(decay[:, :, :, :, 0:1].rearrange("p a m b o -> p (a m b) o"), 0.0).then_inc(dve_init, 1)
            nc.vector.memset(oprev[:, :, 0:1], NEG_INF).then_inc(dve_init, 1)
            nc.vector.memset(decay_row[:, :, :, :], 0.0).then_inc(dve_init, 1)
            dve.wait_ge(ld["vec"], VEC_LOADS * 16)
            dve.wait_ge(dve_init, 4)
            for c in range(CT):
                nc.vector.tensor_scalar(decay_row[:, c], decay_row[:, c], decay_w[:, c:c + 1], None, ALU.add).then_inc(dve_init, 1)
            dve.wait_ge(dve_init, 4 + CT)
            nc.vector.memset(decay_row[:, :, :, 0:1].rearrange("p c b o -> p (c b) o"), NEG_INF).then_inc(dve_init, 1)
            dve.wait_ge(dve_init, INIT_STEPS)
            for k in (*range(7), *range(11, 23)):
                if k == 14:
                    dve.wait_ge(ld["w_ffn"], 16)
                    nc.vector.tensor_reduce(small[:, 0:1], w_ffn.rearrange("p o i -> p (o i)"), AX_X, ALU.add,
                                            apply_absolute_value=True).then_inc(tern_dve, 1)
                if k < 11 or (k - 11) % 3 < 2:
                    front_piece(0, k)
            dve.wait_ge(tern_pe, 1)
            nc.vector.tensor_scalar(small[:, 1:2], psR[:, 0, 0:1], 1.0 / (HID * HID), None, ALU.mult).then_inc(tern_dve, 1)
            for k in range(23, 31):
                front_piece(0, k)
            dve.wait_ge(tern_dve, 2)
            nc.vector.tensor_scalar(small[:, 2:3], small[:, 1:2], TERNARY_EPS, None, ALU.add).then_inc(tern_dve, 1)
            dve.wait_ge(tern_dve, 3)
            nc.vector.reciprocal(small[:, 3:4], small[:, 2:3]).then_inc(tern_dve, 1)
            dve.wait_ge(tern_dve, 4)
            nc.vector.tensor_scalar(w_ffnT[:, :, :], w_ffn, small[:, 3:4], 1.0, ALU.mult, ALU.min).then_inc(tern_dve, 1)
            dve.wait_ge(tern_dve, 5)
            nc.vector.tensor_scalar(w_ffnT[:, :, :], w_ffnT[:, :, :], -1.0, ROUND_MAGIC, ALU.max, ALU.add).then_inc(tern_dve, 1)
            dve.wait_ge(tern_dve, 6)
            nc.vector.tensor_scalar(w_ffnT[:, :, :], w_ffnT[:, :, :], ROUND_MAGIC, small[:, 1:2], ALU.subtract, ALU.mult).then_inc(tern_dve, 1)
            dve.wait_ge(tern_dve, 7)
            nc.vector.tensor_tensor(w_ffnT[:, :, :], w_ffnT[:, :, :], w_ffn, ALU.subtract).then_inc(tern_dve, 1)
            dve.wait_ge(tern_dve, 8)
            nc.vector.tensor_tensor(w_ffnT[:, :, :], w_ffnT[:, :, :], w_ffn, ALU.add).then_inc(tern_dve, 1)
            for h in range(2):
                front_piece(0, 31 + h)
                dve.wait_ge(dt_new, h + 1)
                h = slice(HT * h, HT * h + HT)
                nc.vector.tensor_tensor(dtu[:, :, h], sp_lin[:, :, h], u[:, 0, :, h], ALU.mult).then_inc(dtu_ok, 1)

            def iteration(g, back, front):
                for n in range(NSTATE):
                    for m in range(MT):
                        scan_step(g, n, m)
                        if back:
                            pieces(DVE_BACK, MT * n + m, back_piece, g - 1)
                        if front:
                            pieces(DVE_FRONT, MT * n + m, front_piece, g + 1)

            iteration(0, False, True)
            with dve.Fori(1, GROUPS - 1) as g:
                iteration(g, True, True)
            iteration(GROUPS - 1, True, False)
            for k in (0, 100, 1, 101, *range(2, 35)):
                if k < 100:
                    back_piece(GROUPS - 1, k)
                else:
                    h = slice(HT * (k - 100), HT * (k - 99))
                    dve.wait_ge(skip_ok, 2 * MT * (GROUPS - 1) + MT * (k - 99))
                    nc.vector.tensor_tensor(z[:, :, h], z[:, :, h], gate[:, (GROUPS - 1) % 2, :, h], ALU.mult).then_inc(z_ok, 1)

        @block.gpsimd
        def _(pool):
            def front_piece(g, h):
                hs = slice(HT * h, HT * h + HT)
                pool.wait_ge(dt_new, 2 * g + h + 1)
                nc.gpsimd.tensor_tensor(dtu[:, :, hs], sp_lin[:, :, hs], u[:, g % 2, :, hs], ALU.mult).then_inc(dtu_ok, 1)

            def back_piece(g, k):
                gp = g % 2
                if k < 2:
                    hs = slice(HT * k, HT * k + HT)
                    pool.wait_ge(skip_ok, 2 * MT * g + MT * (k + 1))
                    nc.gpsimd.tensor_tensor(z[:, :, hs], z[:, :, hs], gate[:, gp, :, hs], ALU.mult).then_inc(z_ok, 1)
                elif k == 2:
                    pool.wait_ge(upd_exp, g + 1)
                    pool.wait_ge(ld_ctx, 16 * (g + 1))
                    nc.gpsimd.tensor_tensor(dead_u(gp, 1), ex_upd[:, 1], vT[:, :], ALU.mult).then_inc(ev_upd_ok, 1)
                elif k == 3:
                    pool.wait_ge(out_exp, g + 1)
                    nc.gpsimd.tensor_tensor(dead_gate(gp, 1), ex_out[:, 1], vT[:, :], ALU.mult).then_inc(ev_out_ok, 1)
                elif k == 4:
                    pool.wait_ge(p_ok, g + 1)
                    pool.wait_ge(pq_zero, g + 1)
                    hold_wait(pool)
                    nc.gpsimd.tensor_tensor(dead_gate(gp, 0), ex_out[:, 0], pbuf[:, 0:CT * TOK], ALU.mult).then_inc(num_ok, 1)
                elif k == 5:
                    pool.wait_ge(num_ok, 2 * g + 1)
                    pool.wait_ge(ev_out_ok, g + 1)
                    hold_wait(pool)
                    nc.gpsimd.tensor_tensor(dead_gate(gp, 0), dead_gate(gp, 0), dead_gate(gp, 1), ALU.add).then_inc(num_ok, 1)
                else:
                    tile_read(pool, back_tile(g, B_YT + 1))
                    hold_wait(pool)
                    nc.gpsimd.tensor_tensor(dead_gate(gp, 0).rearrange("p (b c) -> p b c", b=NB), x2[:, :, :],
                                            ffn_bias[:, :].rearrange("p (o c) -> p o c", o=1).broadcast_to((P, NB, HID)),
                                            ALU.add).then_inc(x3b_ok, 1)

            def product_step(g, n):
                pool.wait_ge(ld_c[n % C_RING], 16 * (NSTATE // C_RING * g + n // C_RING + 1))
                s = state[:, n % STATE_RING]
                if n == NSTATE - 1:
                    for m in range(MT):
                        pool.wait_ge(scan_ok, SLOTS * g + MT * n + m + 1)
                        nc.gpsimd.tensor_tensor(s[:, m, :], s[:, m, :], c_rep[:, n % C_RING, :], ALU.mult).then_inc(prod_ok, 1)
                else:
                    for h in (slice(0, MT // 2), slice(MT // 2, MT)):
                        pool.wait_ge(scan_ok, SLOTS * g + MT * n + h.stop)
                        nc.gpsimd.tensor_tensor(s[:, h], s[:, h], c_rep[:, n % C_RING:n % C_RING + 1, :].broadcast_to((P, MT // 2, TOK)),
                                                ALU.mult).then_inc(prod_ok, 1)
                if n in PAIRED:
                    for h in (slice(0, MT // 2), slice(MT // 2, MT)):
                        pool.wait_ge(prod_ok, PRODS * g + 2 * n + h.stop // 2)
                        nc.gpsimd.tensor_tensor(s[:, h], s[:, h], state[:, (n - 1) % STATE_RING, h], ALU.add).then_inc(pair_ok, 1)

            nc.gpsimd.memset(ident[:, :], 0.0).then_inc(pool_init, 1)
            pool.wait_ge(pool_init, 1)
            nc.gpsimd.affine_select(out=ident[:, :], in_=ident[:, :], compare_op=ALU.not_equal, fill=1.0, base=0,
                                    pattern=[[-1, P]], channel_multiplier=1).then_inc(pool_init, 1)
            def iteration(g, back, front):
                for n in range(NSTATE):
                    product_step(g, n)
                    if back:
                        pieces(POOL_BACK, n, back_piece, g - 1)
                    if front:
                        pieces(POOL_FRONT, n, front_piece, g + 1)

            iteration(0, False, True)
            with pool.Fori(1, GROUPS - 1) as g:
                iteration(g, True, True)
            iteration(GROUPS - 1, True, False)
            for k in range(2, 7):
                back_piece(GROUPS - 1, k)


_INS = ["x", "ctx_2048", "L0_attn_in_proj_w", "L0_attn_conv_w", "L0_attn_conv_b", "L0_attn_x_proj_w",
        "L0_attn_dt_proj_w", "L0_attn_dt_proj_b", "L0_attn_A_log", "L0_attn_D", "L0_attn_out_proj_w",
        "L0_xattn_w", "L0_xattn_u", "L0_ffn_weight", "L0_ffn_bias"]

_VECTORS = ["L0_attn_conv_b", "L0_attn_dt_proj_b", "L0_attn_D", "L0_xattn_w", "L0_xattn_u"]


def kernel(**inputs):
    import numpy as np
    from concourse import bacc
    from concourse.bass_utils import run_bass_kernel_spmd

    nc = bacc.Bacc("TRN2", target_bir_lowering=False, num_devices=1)
    arrays, args = {}, []
    for name in _INS:
        a = np.asarray(inputs[name])
        if name == "ctx_2048":
            a = a.transpose(2, 0, 1).reshape(a.shape[2], -1)
        elif name == "L0_ffn_weight":
            a = a.T
        elif name in _VECTORS:
            a = a.reshape(-1, P).T
        a = np.ascontiguousarray(a)
        arrays[f"in_{name}"] = a
        args.append(nc.dram_tensor(f"in_{name}", a.shape, mybir.dt.from_np(a.dtype), kind="ExternalInput").ap())
    shape = tuple(inputs["x"].shape)
    args.append(nc.dram_tensor("out_0", shape, F32, kind="ExternalOutput").ap())
    build_decoder(nc, *args)
    r = run_bass_kernel_spmd(nc, [arrays], core_ids=[0])
    return r.results[0]["out_0"]
```
